# Optimizing a Trainium2 kernel written in Bass

```python
import numpy as np
import jax
import jax.numpy as jnp

def _softmax(x, axis=-1):
    return jax.nn.softmax(x, axis=axis)

def _gelu(x):
    return jax.nn.gelu(x, approximate=True)

def _silu(x):
    return jax.nn.silu(x)

def _sigmoid(x):
    return jax.nn.sigmoid(x)

def _layernorm(x, axis=-1, eps=1e-05):
    m = jnp.mean(x, axis=axis, keepdims=True)
    v = jnp.var(x, axis=axis, keepdims=True)
    return (x - m) / jnp.sqrt(v + eps)

def _scatter_add(tgt, idx, src, axis=0):
    return tgt.at[idx].add(src)

def _segment_sum(src, seg, n):
    return jax.ops.segment_sum(src, seg, n)
kernel_name = 'mk_adaln_d2_jaxref_r8_42ce68'

def setup_inputs(seed: int=0):
    np.random.seed(seed)
    _w = jnp.asarray

    def _L0_attn_setup():
        import jax, jax.numpy as jnp
        import numpy as np
        NEG_BIG = -1e+38

        def _wkv_scan(w, u, k, v, aa0, bb0, pp0):
            kT = jnp.moveaxis(k, 1, 0)
            vT = jnp.moveaxis(v, 1, 0)

            def step(carry, kv):
                aa, bb, pp = carry
                kt, vt = kv
                ww = u + kt
                p = jnp.maximum(pp, ww)
                e1 = jnp.exp(pp - p)
                e2 = jnp.exp(ww - p)
                y = (e1 * aa + e2 * vt) / (e1 * bb + e2)
                ww2 = pp + w
                p2 = jnp.maximum(ww2, kt)
                e1 = jnp.exp(ww2 - p2)
                e2 = jnp.exp(kt - p2)
                return ((e1 * aa + e2 * vt, e1 * bb + e2, p2), y)
            (aa, bb, pp), yT = jax.lax.scan(step, (aa0, bb0, pp0), (kT, vT))
            return (jnp.moveaxis(yT, 0, 1), aa, bb, pp)

        def _reference_tuple_inner(x, W_rvk, W_out, time_decay, time_first):
            B, T, C = x.shape
            rvk = jnp.einsum('btc,dc->btd', x, W_rvk)
            r, v, k = jnp.split(rvk, 3, axis=-1)
            w = -jnp.exp(time_decay)
            u = time_first
            aa0 = jnp.zeros((B, C), dtype=x.dtype)
            bb0 = jnp.zeros((B, C), dtype=x.dtype)
            pp0 = jnp.full((B, C), NEG_BIG, dtype=x.dtype)
            wkv, aa, bb, pp = _wkv_scan(w, u, k, v, aa0, bb0, pp0)
            rwkv = jax.nn.sigmoid(r) * wkv
            out = jnp.einsum('btc,dc->btd', rwkv, W_out)
            h = aa
            c = jnp.stack([bb, pp], axis=-1).reshape(B, 2 * C)
            return (out, h, c)
        key = jax.random.key(seed)
        k1, k2, k3 = jax.random.split(key, 3)
        B, T, C = (32, 128, 128)
        x = jax.random.normal(k1, (B, T, C), dtype=jnp.float32)
        W_rvk = jax.random.normal(k2, (3 * C, C), dtype=jnp.float32) * (1.0 / np.sqrt(C))
        W_out = jax.random.normal(k3, (C, C), dtype=jnp.float32) * (1.0 / np.sqrt(C))
        time_decay = jnp.ones((C,), dtype=jnp.float32)
        time_first = jnp.ones((C,), dtype=jnp.float32)
        return {'x': x, 'W_rvk': W_rvk, 'W_out': W_out, 'time_decay': time_decay, 'time_first': time_first}
    _L0_attn_in = _L0_attn_setup()

    def _L0_ffn_setup():
        import jax, jax.numpy as jnp
        import numpy as np
        B, S, D, E, K = (4, 256, 128, 8, 2)
        H = 4 * D
        key = jax.random.key(seed)
        ks = jax.random.split(key, 8)
        scale = 0.02
        x = jax.random.normal(ks[0], (B, S, D), dtype=jnp.float32)
        Wr = jax.random.normal(ks[1], (D, E), dtype=jnp.float32) * scale
        br = jnp.zeros((E,), dtype=jnp.float32)
        W1 = jax.random.normal(ks[2], (E, D, H), dtype=jnp.float32) * scale
        b1 = jnp.zeros((E, H), dtype=jnp.float32)
        W2 = jax.random.normal(ks[3], (E, H, D), dtype=jnp.float32) * scale
        b2 = jnp.zeros((E, D), dtype=jnp.float32)
        return {'x': x, 'Wr': Wr, 'br': br, 'W1': W1, 'b1': b1, 'W2': W2, 'b2': b2}
    _L0_ffn_in = _L0_ffn_setup()
    _L0_c = _w((lambda *s: np.random.randn(*s).astype(np.float32) * 0.05)(2, 128))
    _L0_wmod = _w((lambda *s: np.random.randn(*s).astype(np.float32) * 0.05)(128, 6 * 128) * 128 ** (-0.5))

    def _L1_attn_setup():
        import jax, jax.numpy as jnp
        import numpy as np
        from jax import lax
        B, T, C, H = (4, 256, 128, 16)
        K = C // H
        E_MIX, E_DEC = (32, 64)
        EPS = 1e-05 * 8 ** 2

        def _rwkv6_tmix(x, time_maa_x, time_maa_w, time_maa_k, time_maa_v, time_maa_r, time_maa_g, maa_w1, maa_w2, time_decay, td_w1, td_w2, u, Wr, Wk, Wv, Wg, Wo, ln_g, ln_b):
            b, t, c = x.shape
            x_prev = jnp.pad(x, ((0, 0), (1, 0), (0, 0)))[:, :t]
            xx = x_prev - x
            mix = jnp.tanh((x + xx * time_maa_x) @ maa_w1).reshape(b, t, 5, E_MIX)
            mix = jnp.einsum('btfe,fec->fbtc', mix, maa_w2)
            mw, mk, mv, mr, mg = mix
            xw = x + xx * (time_maa_w + mw)
            xk = x + xx * (time_maa_k + mk)
            xv = x + xx * (time_maa_v + mv)
            xr = x + xx * (time_maa_r + mr)
            xg = x + xx * (time_maa_g + mg)
            r = xr @ Wr.T
            k = xk @ Wk.T
            v = xv @ Wv.T
            g = jax.nn.silu(xg @ Wg.T)
            w = time_decay + jnp.tanh(xw @ td_w1) @ td_w2
            decay = jnp.exp(-jnp.exp(w))
            to_tbhk = lambda a: a.reshape(b, t, H, K).transpose(1, 0, 2, 3)
            rs, ks_, vs, ds = map(to_tbhk, (r, k, v, decay))

            def step(S, inp):
                r_t, k_t, v_t, d_t = inp
                kv = k_t[..., :, None] * v_t[..., None, :]
                y = jnp.einsum('bhk,bhkj->bhj', r_t, S + u[None, :, :, None] * kv)
                S = d_t[..., None] * S + kv
                return (S, y)
            S0 = jnp.zeros((b, H, K, K), x.dtype)
            _, y = lax.scan(step, S0, (rs, ks_, vs, ds))
            y = y.transpose(1, 0, 2, 3)
            mu = y.mean(-1, keepdims=True)
            var = y.var(-1, keepdims=True)
            y = ((y - mu) / jnp.sqrt(var + EPS)).reshape(b, t, c) * ln_g + ln_b
            return y * g @ Wo.T
        key = jax.random.key(seed)
        ks = jax.random.split(key, 24)
        u01 = lambda k, s: jax.random.uniform(k, s, jnp.float32, -0.01, 0.01)
        nrm = lambda k, s, sc: jax.random.normal(k, s, jnp.float32) * sc
        return {'x': jax.random.normal(ks[0], (B, T, C), jnp.float32), 'time_maa_x': jax.random.uniform(ks[1], (1, 1, C)), 'time_maa_w': jax.random.uniform(ks[2], (1, 1, C)), 'time_maa_k': jax.random.uniform(ks[3], (1, 1, C)), 'time_maa_v': jax.random.uniform(ks[4], (1, 1, C)), 'time_maa_r': jax.random.uniform(ks[5], (1, 1, C)), 'time_maa_g': jax.random.uniform(ks[6], (1, 1, C)), 'maa_w1': u01(ks[7], (C, 5 * E_MIX)), 'maa_w2': u01(ks[8], (5, E_MIX, C)), 'time_decay': jax.random.uniform(ks[9], (1, 1, C), jnp.float32, -6.0, -1.0), 'td_w1': u01(ks[10], (C, E_DEC)), 'td_w2': u01(ks[11], (E_DEC, C)), 'u': nrm(ks[12], (H, K), 0.1), 'Wr': nrm(ks[13], (C, C), 0.02), 'Wk': nrm(ks[14], (C, C), 0.02), 'Wv': nrm(ks[15], (C, C), 0.02), 'Wg': nrm(ks[16], (C, C), 0.02), 'Wo': nrm(ks[17], (C, C), 0.02), 'ln_g': jnp.ones((C,), jnp.float32), 'ln_b': jnp.zeros((C,), jnp.float32)}
    _L1_attn_in = _L1_attn_setup()

    def _L1_ffn_setup():
        import jax, jax.numpy as jnp
        import numpy as np
        B, T, D = (2, 256, 128)
        E, DFF, TOPK = (8, 512, 2)
        TEMPERATURE = 1.0
        key = jax.random.key(seed)
        k_x, k_w1, k_w2, k_r = jax.random.split(key, 4)
        x = jax.random.normal(k_x, (B, T, D), dtype=jnp.float32)
        W1 = jax.random.normal(k_w1, (E, DFF, D), dtype=jnp.float32) * 0.02
        W2 = jax.random.normal(k_w2, (E, D, DFF), dtype=jnp.float32) * 0.02
        Wr = jax.random.normal(k_r, (E, D), dtype=jnp.float32) * 0.02
        return {'x': x, 'W1': W1, 'W2': W2, 'Wr': Wr}
    _L1_ffn_in = _L1_ffn_setup()
    _L1_c = _w((lambda *s: np.random.randn(*s).astype(np.float32) * 0.05)(2, 128))
    _L1_wmod = _w((lambda *s: np.random.randn(*s).astype(np.float32) * 0.05)(128, 6 * 128) * 128 ** (-0.5))
    _d = {'L0_attn_x': _L0_attn_in['x'], 'L0_attn_W_rvk': _L0_attn_in['W_rvk'], 'L0_attn_W_out': _L0_attn_in['W_out'], 'L0_attn_time_decay': _L0_attn_in['time_decay'], 'L0_attn_time_first': _L0_attn_in['time_first'], 'L0_ffn_Wr': _L0_ffn_in['Wr'], 'L0_ffn_br': _L0_ffn_in['br'], 'L0_ffn_W1': _L0_ffn_in['W1'], 'L0_ffn_b1': _L0_ffn_in['b1'], 'L0_ffn_W2': _L0_ffn_in['W2'], 'L0_ffn_b2': _L0_ffn_in['b2'], 'L0_c': _L0_c, 'L0_wmod': _L0_wmod, 'L1_attn_time_maa_x': _L1_attn_in['time_maa_x'], 'L1_attn_time_maa_w': _L1_attn_in['time_maa_w'], 'L1_attn_time_maa_k': _L1_attn_in['time_maa_k'], 'L1_attn_time_maa_v': _L1_attn_in['time_maa_v'], 'L1_attn_time_maa_r': _L1_attn_in['time_maa_r'], 'L1_attn_time_maa_g': _L1_attn_in['time_maa_g'], 'L1_attn_maa_w1': _L1_attn_in['maa_w1'], 'L1_attn_maa_w2': _L1_attn_in['maa_w2'], 'L1_attn_time_decay': _L1_attn_in['time_decay'], 'L1_attn_td_w1': _L1_attn_in['td_w1'], 'L1_attn_td_w2': _L1_attn_in['td_w2'], 'L1_attn_u': _L1_attn_in['u'], 'L1_attn_Wr': _L1_attn_in['Wr'], 'L1_attn_Wk': _L1_attn_in['Wk'], 'L1_attn_Wv': _L1_attn_in['Wv'], 'L1_attn_Wg': _L1_attn_in['Wg'], 'L1_attn_Wo': _L1_attn_in['Wo'], 'L1_attn_ln_g': _L1_attn_in['ln_g'], 'L1_attn_ln_b': _L1_attn_in['ln_b'], 'L1_ffn_W1': _L1_ffn_in['W1'], 'L1_ffn_W2': _L1_ffn_in['W2'], 'L1_ffn_Wr': _L1_ffn_in['Wr'], 'L1_c': _L1_c, 'L1_wmod': _L1_wmod}
    _x0 = _d['L0_attn_x']
    _d['L0_attn_x'] = jax.random.normal(jax.random.fold_in(jax.random.key(seed), 1), (2, 1024, 128), dtype=_x0.dtype)
    del _x0
    return _d

def reference(L0_attn_x, L0_attn_W_rvk, L0_attn_W_out, L0_attn_time_decay, L0_attn_time_first, L0_ffn_Wr, L0_ffn_br, L0_ffn_W1, L0_ffn_b1, L0_ffn_W2, L0_ffn_b2, L0_c, L0_wmod, L1_attn_time_maa_x, L1_attn_time_maa_w, L1_attn_time_maa_k, L1_attn_time_maa_v, L1_attn_time_maa_r, L1_attn_time_maa_g, L1_attn_maa_w1, L1_attn_maa_w2, L1_attn_time_decay, L1_attn_td_w1, L1_attn_td_w2, L1_attn_u, L1_attn_Wr, L1_attn_Wk, L1_attn_Wv, L1_attn_Wg, L1_attn_Wo, L1_attn_ln_g, L1_attn_ln_b, L1_ffn_W1, L1_ffn_W2, L1_ffn_Wr, L1_c, L1_wmod):

    def _L0_attn_ref(x, W_rvk, W_out, time_decay, time_first):
        import jax, jax.numpy as jnp
        import numpy as np
        NEG_BIG = -1e+38

        def _wkv_scan(w, u, k, v, aa0, bb0, pp0):
            kT = jnp.moveaxis(k, 1, 0)
            vT = jnp.moveaxis(v, 1, 0)

            def step(carry, kv):
                aa, bb, pp = carry
                kt, vt = kv
                ww = u + kt
                p = jnp.maximum(pp, ww)
                e1 = jnp.exp(pp - p)
                e2 = jnp.exp(ww - p)
                y = (e1 * aa + e2 * vt) / (e1 * bb + e2)
                ww2 = pp + w
                p2 = jnp.maximum(ww2, kt)
                e1 = jnp.exp(ww2 - p2)
                e2 = jnp.exp(kt - p2)
                return ((e1 * aa + e2 * vt, e1 * bb + e2, p2), y)
            (aa, bb, pp), yT = jax.lax.scan(step, (aa0, bb0, pp0), (kT, vT))
            return (jnp.moveaxis(yT, 0, 1), aa, bb, pp)

        def _reference_tuple_inner(x, W_rvk, W_out, time_decay, time_first):
            B, T, C = x.shape
            rvk = jnp.einsum('btc,dc->btd', x, W_rvk)
            r, v, k = jnp.split(rvk, 3, axis=-1)
            w = -jnp.exp(time_decay)
            u = time_first
            aa0 = jnp.zeros((B, C), dtype=x.dtype)
            bb0 = jnp.zeros((B, C), dtype=x.dtype)
            pp0 = jnp.full((B, C), NEG_BIG, dtype=x.dtype)
            wkv, aa, bb, pp = _wkv_scan(w, u, k, v, aa0, bb0, pp0)
            rwkv = jax.nn.sigmoid(r) * wkv
            out = jnp.einsum('btc,dc->btd', rwkv, W_out)
            h = aa
            c = jnp.stack([bb, pp], axis=-1).reshape(B, 2 * C)
            return (out, h, c)
        return _reference_tuple_inner(x, W_rvk, W_out, time_decay, time_first)[0]

    def _L0_ffn_ref(x, Wr, br, W1, b1, W2, b2):
        import jax, jax.numpy as jnp
        import numpy as np
        B, S, D, E, K = (4, 256, 128, 8, 2)
        H = 4 * D
        b, s, d = x.shape
        xf = x.reshape(-1, d)
        n = xf.shape[0]
        logits = xf @ Wr + br
        probs = jax.nn.softmax(logits, axis=-1)
        topw, topi = jax.lax.top_k(probs, K)
        topw = topw / jnp.sum(topw, axis=-1, keepdims=True)
        gates = jnp.zeros((n, E), dtype=xf.dtype).at[jnp.arange(n)[:, None], topi].add(topw)
        out = jnp.zeros_like(xf)
        for e in range(E):
            h = jax.nn.gelu(xf @ W1[e] + b1[e], approximate=False)
            out = out + gates[:, e:e + 1] * (h @ W2[e] + b2[e])
        return out.reshape(b, s, d)

    def _L1_attn_ref(x, time_maa_x, time_maa_w, time_maa_k, time_maa_v, time_maa_r, time_maa_g, maa_w1, maa_w2, time_decay, td_w1, td_w2, u, Wr, Wk, Wv, Wg, Wo, ln_g, ln_b):
        import jax, jax.numpy as jnp
        import numpy as np
        from jax import lax
        B, T, C, H = (4, 256, 128, 16)
        K = C // H
        E_MIX, E_DEC = (32, 64)
        EPS = 1e-05 * 8 ** 2

        def _rwkv6_tmix(x, time_maa_x, time_maa_w, time_maa_k, time_maa_v, time_maa_r, time_maa_g, maa_w1, maa_w2, time_decay, td_w1, td_w2, u, Wr, Wk, Wv, Wg, Wo, ln_g, ln_b):
            b, t, c = x.shape
            x_prev = jnp.pad(x, ((0, 0), (1, 0), (0, 0)))[:, :t]
            xx = x_prev - x
            mix = jnp.tanh((x + xx * time_maa_x) @ maa_w1).reshape(b, t, 5, E_MIX)
            mix = jnp.einsum('btfe,fec->fbtc', mix, maa_w2)
            mw, mk, mv, mr, mg = mix
            xw = x + xx * (time_maa_w + mw)
            xk = x + xx * (time_maa_k + mk)
            xv = x + xx * (time_maa_v + mv)
            xr = x + xx * (time_maa_r + mr)
            xg = x + xx * (time_maa_g + mg)
            r = xr @ Wr.T
            k = xk @ Wk.T
            v = xv @ Wv.T
            g = jax.nn.silu(xg @ Wg.T)
            w = time_decay + jnp.tanh(xw @ td_w1) @ td_w2
            decay = jnp.exp(-jnp.exp(w))
            to_tbhk = lambda a: a.reshape(b, t, H, K).transpose(1, 0, 2, 3)
            rs, ks_, vs, ds = map(to_tbhk, (r, k, v, decay))

            def step(S, inp):
                r_t, k_t, v_t, d_t = inp
                kv = k_t[..., :, None] * v_t[..., None, :]
                y = jnp.einsum('bhk,bhkj->bhj', r_t, S + u[None, :, :, None] * kv)
                S = d_t[..., None] * S + kv
                return (S, y)
            S0 = jnp.zeros((b, H, K, K), x.dtype)
            _, y = lax.scan(step, S0, (rs, ks_, vs, ds))
            y = y.transpose(1, 0, 2, 3)
            mu = y.mean(-1, keepdims=True)
            var = y.var(-1, keepdims=True)
            y = ((y - mu) / jnp.sqrt(var + EPS)).reshape(b, t, c) * ln_g + ln_b
            return y * g @ Wo.T
        return _rwkv6_tmix(x, time_maa_x, time_maa_w, time_maa_k, time_maa_v, time_maa_r, time_maa_g, maa_w1, maa_w2, time_decay, td_w1, td_w2, u, Wr, Wk, Wv, Wg, Wo, ln_g, ln_b)

    def _L1_ffn_ref(x, W1, W2, Wr):
        import jax, jax.numpy as jnp
        import numpy as np
        B, T, D = (2, 256, 128)
        E, DFF, TOPK = (8, 512, 2)
        TEMPERATURE = 1.0
        logits = jnp.einsum('btd,ed->bte', x, Wr)
        probs = jax.nn.softmax(logits / TEMPERATURE, axis=-1)
        topk_vals, topk_idx = jax.lax.top_k(probs, TOPK)
        router_weights = topk_vals / topk_vals.sum(-1, keepdims=True)
        one_hot = jax.nn.one_hot(topk_idx, E, dtype=x.dtype)
        gate = jnp.einsum('btk,btke->bte', router_weights, one_hot)
        h = jax.nn.silu(jnp.einsum('btd,efd->btef', x, W1))
        y = jnp.einsum('btef,edf->bted', h, W2)
        out = jnp.einsum('bte,bted->btd', gate, y)
        return out
    x = L0_attn_x
    mod = (_silu(L0_c) @ L0_wmod).reshape(L0_c.shape[0], 6, 1, -1)
    sa, ca, ga, sb, cb, gb = (mod[:, 0], mod[:, 1], mod[:, 2], mod[:, 3], mod[:, 4], mod[:, 5])
    ga = (2 * (ga >= 0) - 1) * jnp.maximum(jnp.abs(ga), 0.25)
    gb = (2 * (gb >= 0) - 1) * jnp.maximum(jnp.abs(gb), 0.25)
    h = _layernorm(x, axis=-1) * (1 + ca) + sa
    x = x + ga * _L0_attn_ref(h, L0_attn_W_rvk, L0_attn_W_out, L0_attn_time_decay, L0_attn_time_first)
    h = _layernorm(x, axis=-1) * (1 + cb) + sb
    x = x + gb * _L0_ffn_ref(h, L0_ffn_Wr, L0_ffn_br, L0_ffn_W1, L0_ffn_b1, L0_ffn_W2, L0_ffn_b2)
    mod = (_silu(L1_c) @ L1_wmod).reshape(L1_c.shape[0], 6, 1, -1)
    sa, ca, ga, sb, cb, gb = (mod[:, 0], mod[:, 1], mod[:, 2], mod[:, 3], mod[:, 4], mod[:, 5])
    ga = (2 * (ga >= 0) - 1) * jnp.maximum(jnp.abs(ga), 0.25)
    gb = (2 * (gb >= 0) - 1) * jnp.maximum(jnp.abs(gb), 0.25)
    h = _layernorm(x, axis=-1) * (1 + ca) + sa
    x = x + ga * _L1_attn_ref(h, L1_attn_time_maa_x, L1_attn_time_maa_w, L1_attn_time_maa_k, L1_attn_time_maa_v, L1_attn_time_maa_r, L1_attn_time_maa_g, L1_attn_maa_w1, L1_attn_maa_w2, L1_attn_time_decay, L1_attn_td_w1, L1_attn_td_w2, L1_attn_u, L1_attn_Wr, L1_attn_Wk, L1_attn_Wv, L1_attn_Wg, L1_attn_Wo, L1_attn_ln_g, L1_attn_ln_b)
    h = _layernorm(x, axis=-1) * (1 + cb) + sb
    x = x + gb * _L1_ffn_ref(h, L1_ffn_W1, L1_ffn_W2, L1_ffn_Wr)
    return x

_drawn_inputs = setup_inputs


def setup_inputs(seed=0):
    import zlib

    import numpy as np

    out = dict(_drawn_inputs(seed))
    spreads = {'L0_attn_time_decay': (1.0, 0.6),
     'L0_attn_time_first': (1.0, 0.6),
     'L0_ffn_br': (0.0, 0.478),
     'L0_ffn_b1': (0.0, 0.8),
     'L0_ffn_b2': (0.0, 0.485),
     'L1_attn_ln_g': (1.0, 0.6),
     'L1_attn_ln_b': (0.0, 0.8)}
    factors = {'L0_ffn_Wr': 3.567,
     'L0_ffn_W1': 5.991,
     'L0_ffn_W2': 5.468,
     'L1_attn_time_maa_x': 8.0,
     'L1_attn_time_maa_w': 64.0,
     'L1_attn_time_maa_k': 8.0,
     'L1_attn_time_maa_v': 8.0,
     'L1_attn_time_maa_r': 8.0,
     'L1_attn_time_maa_g': 8.0,
     'L1_attn_maa_w1': 8.0,
     'L1_attn_maa_w2': 8.0,
     'L1_attn_time_decay': 51.977,
     'L1_attn_td_w1': 64.0,
     'L1_attn_td_w2': 64.0,
     'L1_attn_u': 8.0,
     'L1_attn_Wr': 8.0,
     'L1_attn_Wk': 8.0,
     'L1_attn_Wv': 8.0,
     'L1_attn_Wg': 8.0,
     'L1_attn_Wo': 8.0,
     'L1_ffn_W1': 6.057,
     'L1_ffn_W2': 5.868,
     'L1_ffn_Wr': 6.906,
     'L1_c': 5.046,
     'L1_wmod': 5.281}
    for name, (base, spread) in spreads.items():
        noise = np.random.default_rng([zlib.crc32(name.encode()), seed]).standard_normal(out[name].shape)
        drawn = base * np.exp(spread * noise) if base else spread * noise
        out[name] = jnp.asarray(drawn.astype(out[name].dtype))
    for name, factor in factors.items():
        out[name] = (out[name] * factor).astype(out[name].dtype)
    return out
```

```python
from contextlib import ExitStack

import numpy as np

import concourse.bass as bass
from concourse import mybir

F32 = mybir.dt.float32
F32R = mybir.dt.float32r
ALU = mybir.AluOpType
ACT = mybir.ActivationFunctionType
AX_X = mybir.AxisListType.X

P = 128
NB = 2
T = 1024
N = NB * T
BLK = 512
NBLK = N // BLK
BPB = T // BLK
NT = N // P
NE = 8
FH = 512
NC = FH // P
STEPS = NBLK * NC
BODY = 2 * STEPS
RING = 4
LOOK = 2
HK = 8
EMIX = 32
EDEC = 64
LN_EPS = 1e-5
GN_EPS = 1e-5 * 8 ** 2
NEG_BIG = -1e38
GATE_FLOOR = 0.25

C_TD0, C_U0 = 0, 1
C_MAA = 2
C_TD1, C_U1, C_LNG, C_LNB = 8, 9, 10, 11
C_COND = 12
NCOL = 16

MIXES = ("w", "k", "v", "r", "g")


def program(nc, x_d, wrvk_d, wout0_d, cols_d, wmod_d, wp_d, b1_d, b2_d, br_d, wr_d,
            maaw1_d, maaw2_d, tdw1_d, tdw2_d, wproj_d, const_d, out_d, gate_d):
    with ExitStack() as ctx:
        def sb(name, shape, dt=F32):
            return ctx.enter_context(nc.sbuf_tensor(name, shape, dt))

        def sem(name):
            return ctx.enter_context(nc.semaphore(name))

        x = sb("x", [P, N])
        H = sb("H", [P, NB, T + 1])
        h_hi = sb("h_hi", [P, N], F32R)
        h_lo = sb("h_lo", [P, N], F32R)
        w_hi = sb("w_hi", [P, 2, 2 * FH], F32R)
        w_lo = sb("w_lo", [P, 2, 2 * FH], F32R)
        w_raw = sb("w_raw", [P, 2, 2 * FH])
        g_hi = sb("g_hi", [P, RING, BLK], F32R)
        g_lo = sb("g_lo", [P, RING, BLK], F32R)
        sel = sb("sel", [P, HK, P], F32R)
        cols = sb("cols", [P, NCOL])
        wrvk = sb("wrvk", [P, 3 * P])
        wout0 = sb("wout0", [P, P])
        jmean = sb("jmean", [P, P])
        eps = sb("eps", [P, 2])
        mod = sb("mod", [P, 2, 6, NB])
        gate_abs = sb("gate_abs", [P, 2, 2, NB])
        gate_sgn = sb("gate_sgn", [P, 2, 2, NB])
        cond = sb("cond", [P, 2 * NB])
        one_c = sb("one_c", [P, 2, 2, NB])
        gate = sb("gate", [P, 2, 2, NB])
        wdec = sb("wdec", [P, 1])
        b1 = sb("b1", [P, NE * NC])
        b1e = sb("b1e", [P, 2, NC])
        zero = sb("zero", [P, 1])
        b2 = sb("b2", [NE, P])
        br = sb("br", [P, NE])
        wr = sb("wr", [P, 2, NE])
        maaw1 = sb("maaw1", [P, 5 * EMIX])
        maaw2 = sb("maaw2", [P, P])
        maaw2g = sb("maaw2g", [EMIX, P])
        tdw1 = sb("tdw1", [P, EDEC])
        tdw2 = sb("tdw2", [EDEC, P])
        wproj = sb("wproj", [P, 5, P])
        consts = sb("consts", [P, 19, P])
        ident = consts[:, 17, :]
        headones = consts[:, 16, :]
        ranks = consts[:, 18, :].rearrange("p (t e) -> p t e", e=NE)
        headmean = sb("headmean", [P, P])
        small = sb("small", [P, 12, NT])
        sm3 = sb("sm3", [P, 6, NT, NE])

        arena = sb("arena", [P, 27 * T + 8])
        at = [0]

        def view(width):
            a = arena[:, at[0]:at[0] + width]
            at[0] += width
            return a

        xc = view(N)
        sq = view(N)
        ln_end = at[0]
        A0 = []
        for b in range(NB):
            A0.append({k: view(T) for k in ("K", "V", "R", "p", "d1", "d2", "dE1", "dE2")}
                      | {k: view(T + 1) for k in ("pp", "aa", "bb")})
        at[0] = ln_end
        acc = view(N)
        gbc = view(2 * N).rearrange("p (r n) -> p r n", r=2)
        g32 = view(RING * BLK).rearrange("p (r n) -> p r n", r=RING)
        etmp = view(2 * BLK).rearrange("p (r n) -> p r n", r=2)
        gT = view(P)
        g8 = view(N)
        at[0] = ln_end
        A1 = [{k: view(T) for k in ("K", "R", "V", "G", "dec")} for b in range(NB)]
        xx = view(T)
        mixA, mixB = view(T), view(T)
        xf = [view(T), view(T)]
        td1 = view(T)
        S = [view(T + 1), view(T + 1)]
        y0, yy = view(T), view(T)
        kv = [mixA, mixB]
        prod = xf

        PP = ctx.enter_context(nc.psum_tensor("PP", [P, 8, BLK], F32))

        s_x = sem("x_loaded"); s_small = sem("small_loaded"); s_mod_in = sem("mod_loaded")
        s_a0w = sem("attn0_weights_loaded"); s_const = sem("consts_loaded"); s_a1w = sem("attn1_weights_loaded")
        s_set = sem("constants_set")
        s_modps = sem("mod_products"); s_silu = sem("cond_silu"); s_mod = sem("mod_ready"); s_chain = sem("dve_chain")
        s_mean = sem("ln_mean"); s_xc = sem("ln_centred"); s_sq = sem("ln_squared"); s_var = sem("ln_var")
        s_std = sem("ln_std"); s_h = sem("ln_h"); s_hsp = sem("ln_h_split")
        s_xup = sem("x_updated")
        s_kvr = sem("attn0_products"); s_ev0 = sem("attn0_evacuated"); s_pp = sem("attn0_running_max")
        s_arg = sem("attn0_exp_args"); s_argp = sem("attn0_pool_args"); s_exp = sem("attn0_exps")
        s_e2v = sem("attn0_weighted_values"); s_wkv = sem("attn0_wkv"); s_out0 = sem("attn0_out")
        s_wraw = [sem("w_raw_loaded0"), sem("w_raw_loaded1")]
        s_wsp = sem("w_split"); s_b1 = sem("bias1_placed")
        s_logit = sem("logits"); s_lev = sem("logits_shifted"); s_lexp = sem("logits_exp"); s_gate = sem("gates_ready")
        s_gT = sem("gates_turned"); s_gTs = sem("gates_turned_copied"); s_gdram = sem("gates_in_dram")
        s_g8 = sem("gates_rows_loaded"); s_gbc = [sem("gates_broadcast0"), sem("gates_broadcast1")]
        s_p1 = sem("first_products"); s_act = sem("hidden_activated"); s_lo = sem("hidden_low_part")
        s_p2 = sem("second_products"); s_ev = sem("expert_block_read"); s_bias2 = sem("bias2_products")
        s_mx = sem("attn1_proj_products"); s_mxa = sem("attn1_act_read"); s_mxd = sem("attn1_dve_read")
        s_xmx = sem("attn1_mixed_input"); s_xf = sem("attn1_mix_ready")
        s_ruk = sem("attn1_ruk"); s_dec = sem("attn1_decay"); s_acc = sem("expert_sum"); s_vsp = sem("attn1_v_split"); s_q = sem("attn1_q"); s_y0 = sem("attn1_y0")
        s_vb = sem("attn1_v_spread"); s_kv = sem("attn1_kv"); s_S = sem("attn1_state"); s_prod = sem("attn1_r_state")
        s_yps = sem("attn1_y_added"); s_y = sem("attn1_y"); s_gm = sem("gn_mean"); s_gc = sem("gn_centred")
        s_gs = sem("gn_squared"); s_gv = sem("gn_var"); s_gd = sem("gn_std"); s_yn = sem("attn1_gated")
        s_out1 = sem("attn1_out"); s_done = sem("out_stored")

        def blk(ap, i):
            return ap[:, i * BLK:(i + 1) * BLK]

        def h_blk(i):
            b, o = i // BPB, (i % BPB) * BLK
            return H[:, b, 1 + o:1 + o + BLK]

        def pair(i):
            return PP[:, 2 * i:2 * i + 2, :].rearrange("p a n -> p (a n)")

        block = ctx.enter_context(nc.Block())

        SPLIT_LN = {1: 0, 3: NBLK}

        JOBS = [("mixA", "act"), ("mixB", "act"), ("Mw", "dve"), ("Mk", "dve"), ("td1", "act"), ("Mv", "dve"),
                ("k", "act"), ("td2", "act"), ("Mr", "dve"), ("v", "act"), ("Mg", "dve"), ("r", "act"), ("g", "act")]
        NACT = sum(r == "act" for _, r in JOBS)
        NDVE = len(JOBS) - NACT

        def read_count(b, idx):
            who = JOBS[idx][1]
            before = sum(r == who for _, r in JOBS[:idx + 1])
            return (s_mxa, b * NACT + before) if who == "act" else (s_mxd, b * NDVE + before)

        @block.sync
        def _(sp):
            sp.dma_start(x[:], x_d).then_inc(s_x, 16)
            sp.dma_start(cols[:], cols_d).then_inc(s_small, 16)
            sp.dma_start(wrvk[:], wrvk_d).then_inc(s_a0w, 16)
            sp.dma_start(wout0[:], wout0_d).then_inc(s_a0w, 16)
            sp.dma_start(b1[:], b1_d).then_inc(s_small, 16)
            sp.dma_start(b2[:], b2_d).then_inc(s_small, 16)
            sp.dma_start(br[:], br_d.partition_broadcast(P)).then_inc(s_small, 16)
            sp.dma_start(wr[:], wr_d).then_inc(s_small, 16)
            sp.dma_start(consts[:], const_d).then_inc(s_const, 16)
            sp.dma_start(w_raw[:, 0, :], wp_d[0]).then_inc(s_wraw[0], 16)
            sp.dma_start(w_raw[:, 1, :], wp_d[1]).then_inc(s_wraw[1], 16)
            sp.dma_start(maaw1[:], maaw1_d).then_inc(s_a1w, 16)
            sp.dma_start(maaw2[:], maaw2_d[0:P, :]).then_inc(s_a1w, 16)
            sp.dma_start(maaw2g[:], maaw2_d[P:P + EMIX, :]).then_inc(s_a1w, 16)
            sp.dma_start(tdw1[:], tdw1_d).then_inc(s_a1w, 16)
            sp.dma_start(tdw2[:], tdw2_d).then_inc(s_a1w, 16)
            sp.dma_start(wproj[:], wproj_d).then_inc(s_a1w, 16)

            def load_w(m, p):
                sp.wait_ge(s_wsp, 2 * (m - 1))
                sp.dma_start(w_raw[:, p, :], wp_d[bass.ds(m, 1)].rearrange("o p n -> p (o n)")
                             if not isinstance(m, int) else wp_d[m]).then_inc(s_wraw[p], 16)

            def load_g(F, e, p):
                m = NE * F + e
                if not (isinstance(m, int) and m < 2):
                    sp.wait_ge(s_ev, NBLK * (m - 1))
                src = gate_d[F, bass.ds(e, 1), :] if not isinstance(e, int) else gate_d[F, e:e + 1, :]
                sp.dma_start(gbc[:, p, :], src.rearrange("o n -> (o n)").partition_broadcast(P)).then_inc(s_gbc[p], 16)

            def experts(F):
                sp.wait_ge(s_gTs, F + 1)
                sp.dma_start(gate_d[F].rearrange("e (t p) -> (e t) p", p=P), gT).then_inc(s_gdram, 16)
                sp.wait_ge(s_gdram, 16 * (F + 1))
                load_g(F, 0, 0)
                load_g(F, 1, 1)
                if F == 0:
                    sp.dma_start(g8[0:NE, :], gate_d[0]).then_inc(s_g8, 16)
                with sp.Fori(0, NE // 2 - 1) as i:
                    for p in range(2):
                        load_w(NE * F + 2 * i + 2 + p, p)
                        load_g(F, 2 * i + 2 + p, p)
                if F == 0:
                    load_w(NE, 0)
                    load_w(NE + 1, 1)

            experts(0)
            experts(1)
            for i in range(NBLK):
                sp.wait_ge(s_xup, 3 * NBLK + i + 1)
                sp.dma_start(blk(out_d, i), blk(x, i)).then_inc(s_done, 16)
            sp.wait_ge(s_done, 16 * NBLK)

        @block.gpsimd
        def _(pool):
            pool.memset(jmean[:], 1.0 / P).then_inc(s_set, 1)
            pool.memset(zero[:], 0.0).then_inc(s_set, 1)
            pool.memset(eps[:, 0:1], LN_EPS).then_inc(s_set, 1)
            pool.memset(eps[:, 1:2], GN_EPS).then_inc(s_set, 1)
            pool.memset(H[:, :, 0:1], 0.0).then_inc(s_set, 1)
            pool.wait_ge(s_const, 16)
            pool.tensor_copy(sel[:], consts[:, 0:HK, :]).then_inc(s_set, 1)
            pool.tensor_scalar(headmean[:], headones, 1.0 / HK, None, ALU.mult).then_inc(s_set, 1)

            pool.wait_ge(s_set, 7)

            def split_w(m, p, k):
                pool.wait_ge(s_wraw[p], 16 * (k + 1))
                if not (isinstance(m, int) and m < 2):
                    pool.wait_ge(s_p2, STEPS * (m - 1))
                pool.tensor_tensor(w_hi[:, p, :], w_raw[:, p, :], zero[:, 0:1].broadcast_to([P, 2 * FH]), ALU.add).then_inc(s_wsp, 1)
                pool.wait_ge(s_wsp, 2 * m + 1)
                pool.tensor_tensor(w_lo[:, p, :], w_raw[:, p, :], w_hi[:, p, :].bitcast(F32), ALU.subtract).then_inc(s_wsp, 1)

            def attn0(b):
                A = A0[b]
                pool.wait_ge(s_ev0, 3 * b + 1)
                pool.wait_ge(s_pp, b + 1)
                pool.tensor_tensor(A["dE2"], A["K"], A["pp"][:, 1:T + 1], ALU.subtract).then_inc(s_argp, 1)

            def attn0_v(b):
                A = A0[b]
                pool.wait_ge(s_exp, 4 * b + 2)
                pool.wait_ge(s_arg, 3 * b + 3)
                pool.tensor_tensor(A["K"], A["dE2"], A["V"], ALU.mult).then_inc(s_e2v, 1)
                pool.wait_ge(s_exp, 4 * b + 4)
                pool.tensor_tensor(A["p"], A["d2"], A["V"], ALU.mult).then_inc(s_e2v, 1)

            for b in range(NB):
                attn0(b)
            for b in range(NB):
                attn0_v(b)
            split_w(0, 0, 0)
            split_w(1, 1, 0)
            with pool.Fori(0, NE // 2 - 1) as i:
                for p in range(2):
                    split_w(2 * i + 2 + p, p, i + 1)
            split_w(NE, 0, NE // 2)
            split_w(NE + 1, 1, NE // 2)
            for b in range(NB):
                for j in range(HK):
                    n = b * HK + j
                    pool.wait_ge(s_S, n + 1)
                    if n >= 2:
                        pool.wait_ge(s_yps, n - 1)
                    pool.tensor_tensor(prod[j % 2], A1[b]["R"], S[j % 2][:, 0:T], ALU.mult).then_inc(s_prod, 1)
            with pool.Fori(0, NE // 2 - 1) as i:
                for p in range(2):
                    split_w(NE + 2 * i + 2 + p, p, i + NE // 2 + 1)


        @block.scalar
        def _(act):
            act.dma_start(H[:, :, 1:1 + 6 * P], wmod_d).then_inc(s_mod_in, 16)
            act.wait_ge(s_small, 16 * 5)
            act.activation(cond[:], cols[:, C_COND:C_COND + 2 * NB], ACT.Silu).then_inc(s_silu, 1)
            act.activation(wdec[:], cols[:, C_TD0:C_TD0 + 1], ACT.Exp).then_inc(s_silu, 1)

            def layer_norm(l):
                def square(i):
                    act.wait_ge(s_xc, NBLK * l + i + 1)
                    act.activation(blk(sq, i), blk(xc, i), ACT.Square).then_inc(s_sq, 1)

                def deviation(i):
                    act.wait_ge(s_var, NBLK * l + i + 1)
                    act.activation(blk(sq, i), PP[:, 6 + i % 2, :], ACT.Sqrt, bias=eps[:, 0:1]).then_inc(s_std, 1)

                act.wait_ge(s_set, 3)
                square(0)
                square(1)
                deviation(0)
                square(2)
                deviation(1)
                square(3)
                deviation(2)
                deviation(3)

            def attn0():
                for b in range(NB):
                    for n, (name, func) in enumerate((("K", ACT.Copy), ("V", ACT.Copy), ("R", ACT.Sigmoid))):
                        act.wait_ge(s_kvr, 3 * b + n + 1)
                        act.activation(A0[b][name], pair(n), func).then_inc(s_ev0, 1)
                for b in range(NB):
                    A = A0[b]
                    for n, name in enumerate(("dE1", "dE2", "d1", "d2")):
                        if name == "dE2":
                            act.wait_ge(s_argp, b + 1)
                        else:
                            act.wait_ge(s_arg, 3 * b + {"dE1": 1, "d1": 2, "d2": 3}[name])
                        act.activation(A[name], A[name], ACT.Exp).then_inc(s_exp, 1)

            def experts(F):
                act.wait_ge(s_lev, F + 1)
                act.activation(sm3[:, 1, :, :], sm3[:, 0, :, :], ACT.Exp).then_inc(s_lexp, 1)

                def step(n, s, e):
                    act.wait_ge(s_p1, n + 1)
                    if not (isinstance(n, int) and n < RING):
                        act.wait_ge(s_p2, n - RING + 1)
                        act.wait_ge(s_lo, n - RING + 1)
                    kw = {}
                    if F == 0:
                        p = (s // STEPS) % 2
                        if s % STEPS == 0:
                            act.activation(b1e[:, p, :], b1[:, bass.ds(e * NC, NC)], ACT.Copy).then_inc(s_b1, 1)
                        act.wait_ge(s_b1, e + 1)
                        kw = dict(bias=b1e[:, p, s % NC:s % NC + 1])
                    func = ACT.Gelu if F == 0 else ACT.Silu
                    act.activation(g32[:, s % RING, :], PP[:, s % RING, :], func, **kw).then_inc(s_act, 1)
                    act.activation(g_hi[:, s % RING, :], PP[:, s % RING, :], func, **kw).then_inc(s_act, 1)

                def body(i):
                    for s in range(BODY):
                        step(NE * STEPS * F + BODY * i + s, s, 2 * i + s // STEPS)

                body(0)
                with act.Fori(1, NE // 2) as i:
                    body(i)

            def attn1_proj(b):
                for idx, (name, reader) in enumerate(JOBS):
                    if reader != "act":
                        continue
                    J = b * len(JOBS) + idx
                    src = pair(J % 4)
                    act.wait_ge(s_mx, J + 1)
                    if name == "mixA":
                        act.activation(mixA, src, ACT.Tanh).then_inc(s_mxa, 1)
                    elif name == "mixB":
                        act.activation(mixB[0:EMIX], src[0:EMIX], ACT.Tanh).then_inc(s_mxa, 1)
                    elif name == "td1":
                        act.activation(td1[0:EDEC], src[0:EDEC], ACT.Tanh).then_inc(s_mxa, 1)
                    elif name == "td2":
                        act.activation(A1[b]["dec"], src, ACT.Exp, bias=cols[:, C_TD1:C_TD1 + 1]).then_inc(s_mxa, 1)
                        act.wait_ge(*read_count(b, idx))
                        act.activation(A1[b]["dec"], A1[b]["dec"], ACT.Exp, scale=-1.0).then_inc(s_dec, 1)
                    elif name == "g":
                        act.activation(A1[b]["G"], src, ACT.Silu).then_inc(s_mxa, 1)
                    else:
                        act.activation(A1[b][name.upper()], src, ACT.Copy).then_inc(s_mxa, 1)

            def group_norm(b):
                act.wait_ge(s_gc, b + 1)
                act.activation(yy, y0, ACT.Square).then_inc(s_gs, 1)
                act.wait_ge(s_gv, b + 1)
                act.activation(yy, pair(2), ACT.Sqrt, bias=eps[:, 1:2]).then_inc(s_gd, 1)

            layer_norm(0)
            attn0()
            layer_norm(1)
            experts(0)
            layer_norm(2)
            for b in range(NB):
                attn1_proj(b)
            act.wait_ge(s_set, 4)
            for b in range(NB):
                group_norm(b)
            layer_norm(3)
            experts(1)

        @block.tensor
        def _(pe):
            pe.wait_ge(s_silu, 1)
            pe.wait_ge(s_mod_in, 16)
            for l in range(2):
                for j in range(6):
                    at0 = (l * 6 + j) * NB
                    last = pe.matmul(PP[:, 0, at0:at0 + NB], H[:, l, 1 + j * P:1 + (j + 1) * P],
                                     cond[:, l * NB:(l + 1) * NB], start=True, stop=True)
            last.then_inc(s_modps, 1)

            def layer_norm(l):
                def mean(i):
                    if l == 0:
                        pe.wait_ge(s_x, 16)
                        pe.wait_ge(s_set, 1)
                    else:
                        pe.wait_ge(s_xup, NBLK * (l - 1) + i + 1)
                    if i >= 2:
                        pe.wait_ge(s_xc, NBLK * l + i - 1)
                    pe.matmul(PP[:, 4 + i % 2, :], jmean[:], blk(x, i), start=True, stop=True).then_inc(s_mean, 1)

                def var(i):
                    if l == 1 and i < 2:
                        pe.wait_ge(s_xup, NBLK)
                    if i >= 2:
                        pe.wait_ge(s_std, NBLK * l + i - 1)
                    pe.wait_ge(s_sq, NBLK * l + i + 1)
                    pe.matmul(PP[:, 6 + i % 2, :], jmean[:], blk(sq, i), start=True, stop=True).then_inc(s_var, 1)

                mean(0)
                mean(1)
                var(0)
                mean(2)
                var(1)
                mean(3)
                var(2)
                var(3)

            def attn0():
                pe.wait_ge(s_a0w, 32)
                pe.wait_ge(s_mod, 1)
                for b in range(NB):
                    pe.wait_ge(s_h, BPB * (b + 1))
                    for n, at0 in enumerate((2 * P, P, 0)):
                        if b:
                            pe.wait_ge(s_ev0, n + 1)
                        elif n == 2:
                            pe.wait_ge(s_xc, NBLK)
                        for i in range(BPB):
                            last = pe.matmul(PP[:, 2 * n + i, :], wrvk[:, at0:at0 + P], h_blk(BPB * b + i),
                                             start=True, stop=True)
                        last.then_inc(s_kvr, 1)
                pe.wait_ge(s_std, NBLK)
                for b in range(NB):
                    pe.wait_ge(s_wkv, b + 1)
                    if b:
                        pe.wait_ge(s_xup, BPB)
                    for i in range(BPB):
                        pe.matmul(PP[:, 6 + i, :], wout0[:], blk(A0[b]["p"], i), start=True, stop=True).then_inc(s_out0, 1)

            def experts(F):
                l = 2 * F + 1
                pe.wait_ge(s_h, NBLK * (l + 1))
                pe.wait_ge(s_std, NBLK * (l + 1))
                pe.wait_ge(s_small, 16 * 5)
                for t in range(NT):
                    b, o = t // (NT // NB), (t % (NT // NB)) * P
                    last = pe.matmul(PP[:, 6, t * NE:(t + 1) * NE], H[:, b, 1 + o:1 + o + P], wr[:, F, :],
                                     start=True, stop=True)
                last.then_inc(s_logit, 1)

                def body(i, last=False):
                    m0 = NE * F + 2 * i
                    for s in range(BODY):
                        if not (last and s + LOOK >= BODY):
                            stage1(m0, s + LOOK)
                        stage2(m0, s)

                def stage1(m0, s):
                    p, st = (s // STEPS) % 2, s % STEPS
                    i, c = st // NC, st % NC
                    n = m0 * STEPS + s
                    if st == 0:
                        pe.wait_ge(s_wsp, 2 * (m0 + s // STEPS + 1))
                    if c == 0:
                        pe.wait_ge(s_hsp, 2 * (NBLK * F + i + 1))
                    if not (isinstance(n, int) and n < RING):
                        pe.wait_ge(s_act, 2 * (n - RING + 1))
                    w = slice(c * P, (c + 1) * P)
                    ps = PP[:, s % RING, :]
                    pe.matmul(ps, w_lo[:, p, w], blk(h_hi, i), start=True, stop=False)
                    pe.matmul(ps, w_hi[:, p, w], blk(h_lo, i), start=False, stop=False)
                    pe.matmul(ps, w_hi[:, p, w], blk(h_hi, i), start=False, stop=True).then_inc(s_p1, 1)

                def stage2(m0, s):
                    p, st = (s // STEPS) % 2, s % STEPS
                    c, q = st % NC, s // NC
                    n = m0 * STEPS + s
                    if c == 0 and not (isinstance(n, int) and n < 2 * NC):
                        pe.wait_ge(s_ev, m0 * NBLK + q - 1)
                    pe.wait_ge(s_act, 2 * (n + 1))
                    pe.wait_ge(s_lo, n + 1)
                    w = slice(FH + c * P, FH + (c + 1) * P)
                    ps = PP[:, 4 + q % 2, :]
                    pe.matmul(ps, w_lo[:, p, w], g_hi[:, s % RING, :], start=(c == 0), stop=False)
                    pe.matmul(ps, w_hi[:, p, w], g_lo[:, s % RING, :], start=False, stop=False)
                    pe.matmul(ps, w_hi[:, p, w], g_hi[:, s % RING, :], start=False, stop=(c == NC - 1)).then_inc(s_p2, 1)

                for s in range(LOOK):
                    stage1(NE * F, s)
                pe.wait_ge(s_gate, F + 1)
                pe.wait_ge(s_const, 16)
                pe.transpose(PP[:, 7, 0:P], sm3[:, 5, :, :].rearrange("p t e -> p (t e)"), ident).then_inc(s_gT, 1)
                body(0)
                with pe.Fori(1, NE // 2 - 1) as i:
                    body(i)
                body(NE // 2 - 1, last=True)
                if F == 0:
                    pe.wait_ge(s_g8, 16)
                    pe.wait_ge(s_act, 2 * NE * STEPS)
                    for i in range(NBLK):
                        pe.matmul(PP[:, i, :], b2[:], blk(g8, i)[0:NE], start=True, stop=True).then_inc(s_bias2, 1)

            def attn1_proj(b):
                for idx, (name, reader) in enumerate(JOBS):
                    J = b * len(JOBS) + idx
                    if J >= 4:
                        pe.wait_ge(*read_count((J - 4) // len(JOBS), (J - 4) % len(JOBS)))
                    rows = P
                    if name in ("mixA", "mixB"):
                        pe.wait_ge(s_xmx, b + 1)
                        lhs, src = (maaw1[:, 0:P], y0) if name == "mixA" else (maaw1[:, P:5 * EMIX], y0)
                        rows = P if name == "mixA" else EMIX
                    elif name[0] == "M":
                        f = MIXES.index(name[1])
                        if f < 4:
                            pe.wait_ge(*read_count(b, 0))
                            lhs, src = maaw2[f * EMIX:(f + 1) * EMIX, :], mixA[f * EMIX:(f + 1) * EMIX]
                        else:
                            pe.wait_ge(*read_count(b, 1))
                            lhs, src = maaw2g[:], mixB[0:EMIX]
                    elif name == "td1":
                        pe.wait_ge(s_xf, 5 * b + 1)
                        lhs, src, rows = tdw1[:], xf[0], EDEC
                    elif name == "td2":
                        pe.wait_ge(*read_count(b, 4))
                        lhs, src = tdw2[:], td1[0:EDEC]
                    else:
                        f = MIXES.index(name)
                        pe.wait_ge(s_xf, 5 * b + f + 1)
                        lhs, src = wproj[:, {"k": 0, "v": 1, "r": 2, "g": 3}[name], :], xf[f % 2]
                    for i in range(BPB):
                        last = pe.matmul(PP[0:rows, 2 * (J % 4) + i, :], lhs, blk(src, i), start=True, stop=True)
                    last.then_inc(s_mx, 1)

            def attn1_state(b):
                pe.wait_ge(s_ruk, b + 1)
                for i in range(BPB):
                    last = pe.matmul(PP[:, 6 + i, :], headones, blk(yy, i), start=True, stop=True)
                last.then_inc(s_q, 1)

                def spread(j):
                    n = b * HK + j
                    if n >= 2:
                        pe.wait_ge(s_kv, n - 1)
                    if b and j == 0:
                        pe.wait_ge(s_xup, 2 * NBLK + BPB)
                    for i in range(BPB):
                        at0 = PP[:, 2 * (j % 2) + i, :]
                        pe.matmul(at0, sel[:, j, :], blk(h_lo, BPB * b + i), start=True, stop=False)
                        last = pe.matmul(at0, sel[:, j, :], blk(h_hi, BPB * b + i), start=False, stop=True)
                    last.then_inc(s_vb, 1)

                def gather(j):
                    pe.wait_ge(s_prod, b * HK + j + 1)
                    for i in range(BPB):
                        last = pe.matmul(PP[:, 4 + i, :], consts[:, HK + j, :], blk(prod[j % 2], i),
                                         start=(j == 0), stop=(j == HK - 1), skip_group_check=True)
                    last.then_inc(s_yps, 1)

                pe.wait_ge(s_vsp, 2 * (b + 1))
                spread(0)
                spread(1)
                for j in range(HK):
                    if 2 <= j + 1 < HK:
                        spread(j + 1)
                    gather(j)

            def group_norm(b):
                pe.wait_ge(s_y0, b + 1)
                pe.wait_ge(s_y, b + 1)
                for i in range(BPB):
                    last = pe.matmul(PP[:, 6 + i, :], headmean[:], blk(yy, i), start=True, stop=True)
                last.then_inc(s_gm, 1)
                pe.wait_ge(s_gs, b + 1)
                for i in range(BPB):
                    last = pe.matmul(PP[:, 4 + i, :], headmean[:], blk(yy, i), start=True, stop=True)
                last.then_inc(s_gv, 1)
                pe.wait_ge(s_yn, b + 1)
                for i in range(BPB):
                    pe.matmul(PP[:, i, :], wproj[:, 4, :], blk(y0, i), start=True, stop=True).then_inc(s_out1, 1)

            layer_norm(0)
            attn0()
            layer_norm(1)
            experts(0)
            layer_norm(2)
            pe.wait_ge(s_a1w, 16 * 6)
            pe.wait_ge(s_set, 7)
            pe.wait_ge(s_std, 3 * NBLK)
            for b in range(NB):
                attn1_proj(b)
            pe.wait_ge(s_mxa, NB * NACT)
            pe.wait_ge(s_mxd, NB * NDVE)
            for b in range(NB):
                attn1_state(b)
                group_norm(b)
            layer_norm(3)
            experts(1)

        @block.vector
        def _(dve):
            chain = [0]

            def link(ins):
                chain[0] += 1
                ins.then_inc(s_chain, 1)
                dve.wait_ge(s_chain, chain[0])

            def col(c):
                return cols[:, c:c + 1]

            dve.wait_ge(s_modps, 1)
            link(dve.tensor_copy(mod[:].rearrange("p l j b -> p (l j b)"), PP[:, 0, 0:2 * 6 * NB]))
            for l in range(2):
                sc, ga = mod[:, l, 1:6:3, :], mod[:, l, 2:6:3, :]
                dve.tensor_scalar(one_c[:, l], sc, 1.0, None, ALU.add).then_inc(s_mod, 1)
                link(dve.tensor_scalar(gate_sgn[:, l], ga, 0.0, 2.0, ALU.is_ge, ALU.mult))
                link(dve.tensor_scalar(gate_sgn[:, l], gate_sgn[:, l], -1.0, None, ALU.add))
                link(dve.tensor_tensor(gate_abs[:, l], gate_sgn[:, l], ga, ALU.mult))
                dve.scalar_tensor_tensor(gate[:, l], gate_abs[:, l], GATE_FLOOR, gate_sgn[:, l], ALU.max, ALU.mult).then_inc(s_mod, 1)
            dve.wait_ge(s_silu, 2)
            link(dve.tensor_scalar(wdec[:], wdec[:], -1.0, None, ALU.mult))
            dve.wait_ge(s_mod, 4)

            def layer_norm(l):
                half = l % 2
                L = l // 2

                def centre(i):
                    dve.wait_ge(s_mean, NBLK * l + i + 1)
                    dve.tensor_tensor(blk(xc, i), blk(x, i), PP[:, 4 + i % 2, :], ALU.subtract).then_inc(s_xc, 1)

                def finish(i):
                    b = i // BPB
                    dve.wait_ge(s_std, NBLK * l + i + 1)
                    link(dve.reciprocal(blk(sq, i), blk(sq, i)))
                    link(dve.scalar_tensor_tensor(blk(xc, i), blk(xc, i), one_c[:, L, half, b:b + 1], blk(sq, i),
                                                  ALU.mult, ALU.mult))
                    dve.tensor_scalar(h_blk(i), blk(xc, i), mod[:, L, 3 * half, b:b + 1], None, ALU.add).then_inc(s_h, 1)
                    if half:
                        dve.wait_ge(s_h, NBLK * l + i + 1)
                        dve.tensor_copy(blk(h_hi, i), h_blk(i)).then_inc(s_hsp, 1)
                        dve.wait_ge(s_hsp, 2 * (NBLK * L + i) + 1)
                        dve.tensor_tensor(blk(h_lo, i), h_blk(i), blk(h_hi, i).bitcast(F32), ALU.subtract).then_inc(s_hsp, 1)

                centre(0)
                centre(1)
                finish(0)
                centre(2)
                finish(1)
                centre(3)
                finish(2)
                finish(3)

            def attn0():
                for b in range(NB):
                    A = A0[b]
                    dve.memset(A["pp"][:, 0:1], NEG_BIG)
                    dve.memset(A["aa"][:, 0:1], 0.0)
                    link(dve.memset(A["bb"][:, 0:1], 0.0))
                for b in range(NB):
                    A = A0[b]
                    prev = A["pp"][:, 0:T]
                    dve.wait_ge(s_ev0, 3 * b + 1)
                    dve.tensor_tensor_scan(A["pp"][:, 1:T + 1], wdec[:, 0:1].broadcast_to([P, T]), A["K"], NEG_BIG,
                                           ALU.add, ALU.max).then_inc(s_pp, 1)
                    dve.wait_ge(s_pp, b + 1)
                    dve.scalar_tensor_tensor(A["dE1"], prev, wdec[:, 0:1], A["pp"][:, 1:T + 1], ALU.add,
                                             ALU.subtract).then_inc(s_arg, 1)
                    link(dve.scalar_tensor_tensor(A["p"], A["K"], col(C_U0), prev, ALU.add, ALU.max))
                    dve.tensor_tensor(A["d1"], prev, A["p"], ALU.subtract).then_inc(s_arg, 1)
                    dve.scalar_tensor_tensor(A["d2"], A["K"], col(C_U0), A["p"], ALU.add, ALU.subtract).then_inc(s_arg, 1)
                for b in range(NB):
                    A = A0[b]
                    dve.wait_ge(s_exp, 4 * b + 2)
                    link(dve.tensor_tensor_scan(A["bb"][:, 1:T + 1], A["dE1"], A["dE2"], 0.0, ALU.mult, ALU.add))
                    dve.wait_ge(s_e2v, 2 * b + 1)
                    link(dve.tensor_tensor_scan(A["aa"][:, 1:T + 1], A["dE1"], A["K"], 0.0, ALU.mult, ALU.add))
                    dve.wait_ge(s_exp, 4 * b + 4)
                    link(dve.tensor_tensor(A["dE1"], A["d1"], A["bb"][:, 0:T], ALU.mult))
                    link(dve.tensor_tensor(A["dE1"], A["dE1"], A["d2"], ALU.add))
                    link(dve.reciprocal(A["dE1"], A["dE1"]))
                    link(dve.tensor_tensor(A["d1"], A["d1"], A["aa"][:, 0:T], ALU.mult))
                    dve.wait_ge(s_e2v, 2 * b + 2)
                    link(dve.tensor_tensor(A["d1"], A["d1"], A["p"], ALU.add))
                    link(dve.tensor_tensor(A["d1"], A["d1"], A["dE1"], ALU.mult))
                    dve.wait_ge(s_ev0, 3 * b + 3)
                    dve.tensor_tensor(A["p"], A["d1"], A["R"], ALU.mult).then_inc(s_wkv, 1)
                for b in range(NB):
                    for i in range(BPB):
                        k = BPB * b + i
                        dve.wait_ge(s_out0, k + 1)
                        dve.scalar_tensor_tensor(blk(x, k), PP[:, 6 + i, :], gate[:, 0, 0, b:b + 1], blk(x, k),
                                                 ALU.mult, ALU.add).then_inc(s_xup, 1)

            def over_experts(k):
                return small[:, k, :].unsqueeze(2).broadcast_to([P, NT, NE])

            def route(F):
                logits = PP[:, 6, 0:NT * NE].rearrange("p (t e) -> p t e", e=NE)
                dve.wait_ge(s_logit, F + 1)
                if F == 0:
                    link(dve.tensor_tensor(sm3[:, 0], logits, br[:].unsqueeze(1).broadcast_to([P, NT, NE]), ALU.add))
                else:
                    link(dve.tensor_copy(sm3[:, 0], logits))
                link(dve.tensor_reduce(small[:, 0, :], sm3[:, 0], AX_X, ALU.max))
                dve.tensor_tensor(sm3[:, 0], sm3[:, 0], over_experts(0), ALU.subtract).then_inc(s_lev, 1)
                dve.wait_ge(s_lexp, F + 1)
                link(dve.tensor_reduce(small[:, 1, :], sm3[:, 1], AX_X, ALU.add))
                link(dve.reciprocal(small[:, 2, :], small[:, 1, :]))
                link(dve.tensor_tensor(sm3[:, 0], sm3[:, 1], over_experts(2), ALU.mult))

                def pick(k, onehot):
                    link(dve.tensor_reduce(small[:, k, :], sm3[:, 0], AX_X, ALU.max))
                    link(dve.tensor_tensor(sm3[:, 2], sm3[:, 0], over_experts(k), ALU.is_equal))
                    link(dve.tensor_tensor(sm3[:, 2], sm3[:, 2], ranks, ALU.mult))
                    link(dve.tensor_reduce(small[:, k + 1, :], sm3[:, 2], AX_X, ALU.max))
                    link(dve.tensor_tensor(sm3[:, onehot], sm3[:, 2], over_experts(k + 1), ALU.is_equal))

                dve.wait_ge(s_const, 16)
                pick(3, 3)
                link(dve.scalar_tensor_tensor(sm3[:, 0], sm3[:, 3], -2.0, sm3[:, 0], ALU.mult, ALU.add))
                pick(5, 4)
                link(dve.tensor_tensor(small[:, 7, :], small[:, 3, :], small[:, 5, :], ALU.add))
                link(dve.reciprocal(small[:, 8, :], small[:, 7, :]))
                link(dve.tensor_tensor(small[:, 9, :], small[:, 3, :], small[:, 8, :], ALU.mult))
                link(dve.tensor_tensor(small[:, 10, :], small[:, 5, :], small[:, 8, :], ALU.mult))
                link(dve.tensor_tensor(sm3[:, 3], sm3[:, 3], over_experts(9), ALU.mult))
                link(dve.tensor_tensor(sm3[:, 4], sm3[:, 4], over_experts(10), ALU.mult))
                gout = sm3[:, 5].rearrange("p t e -> p (t e)").rearrange("p (e t) -> p t e", t=NT)
                dve.tensor_tensor(gout, sm3[:, 3], sm3[:, 4], ALU.add).then_inc(s_gate, 1)
                dve.wait_ge(s_gT, F + 1)
                dve.tensor_copy(gT, PP[:, 7, 0:P]).then_inc(s_gTs, 1)

            def experts(F):
                dve.memset(acc, 0.0).then_inc(s_acc, 1)
                route(F)
                nq = NE * NBLK

                def low(n, s):
                    dve.wait_ge(s_act, 2 * (n + 1))
                    if not (isinstance(n, int) and n < RING):
                        dve.wait_ge(s_p2, n - RING + 1)
                    dve.tensor_tensor(g_lo[:, s % RING, :], g32[:, s % RING, :], g_hi[:, s % RING, :].bitcast(F32),
                                      ALU.subtract).then_inc(s_lo, 1)

                def read_block(q0, r, bodies=None):
                    i, p = r % NBLK, (r // NBLK) % 2
                    dve.wait_ge(s_p2, NC * (q0 + r + 1))
                    if i == 0:
                        dve.wait_ge(s_gbc[p], 16 * (bodies + 1))
                    dve.tensor_tensor(etmp[:, r % 2, :], PP[:, 4 + r % 2, :], blk(gbc[:, p, :], i), ALU.mult).then_inc(s_ev, 1)

                def add_block(q0, r):
                    i = r % NBLK
                    dve.wait_ge(s_ev, q0 + r + 1)
                    dve.wait_ge(s_acc, q0 + r - NBLK + 1 + 1 + F if not (isinstance(q0, int) and (q0 + r) % nq < NBLK)
                                else F * (nq + 1) + 1)
                    dve.tensor_tensor(blk(acc, i), blk(acc, i), etmp[:, r % 2, :], ALU.add).then_inc(s_acc, 1)

                def body(i, first=False):
                    n0 = NE * STEPS * F + BODY * i
                    q0 = nq * F + 2 * NBLK * i
                    for s in range(BODY):
                        low(n0 + s, s)
                        if s % NC == 1 and not (first and s == 1):
                            read_block(q0, s // NC - 1, NE // 2 * F + i)
                        if s % NC == 2 and not (first and s == 2):
                            add_block(q0, s // NC - 1)

                body(0, first=True)
                with dve.Fori(1, NE // 2) as i:
                    body(i)
                read_block(nq * (F + 1), -1)
                add_block(nq * (F + 1), -1)
                dve.wait_ge(s_acc, (nq + 1) * (F + 1))
                for i in range(NBLK):
                    b = i // BPB
                    if F == 0:
                        dve.wait_ge(s_bias2, i + 1)
                        link(dve.tensor_tensor(blk(acc, i), blk(acc, i), PP[:, i, :], ALU.add))
                    dve.scalar_tensor_tensor(blk(x, i), blk(acc, i), gate[:, F, 1, b:b + 1], blk(x, i),
                                             ALU.mult, ALU.add).then_inc(s_xup, 1)

            def attn1_proj(b):
                h, hprev = H[:, b, 1:T + 1], H[:, b, 0:T]
                dve.wait_ge(s_h, 2 * NBLK + BPB * (b + 1))
                link(dve.tensor_tensor(xx, hprev, h, ALU.subtract))
                if b:
                    dve.wait_ge(s_mx, len(JOBS) * (b - 1) + 2)
                dve.scalar_tensor_tensor(y0, xx, col(C_MAA), h, ALU.mult, ALU.add).then_inc(s_xmx, 1)
                names = [n for n, _ in JOBS]
                users = [names.index(n) for n in ("td1", "k", "v", "r", "g")]
                for f in range(5):
                    idx = names.index("M" + MIXES[f])
                    if f >= 2:
                        dve.wait_ge(s_mx, len(JOBS) * b + users[f - 2] + 1)
                    elif b:
                        dve.wait_ge(s_mx, len(JOBS) * (b - 1) + users[4 if f == 0 else 3] + 1)
                    J = len(JOBS) * b + idx
                    dve.wait_ge(s_mx, J + 1)
                    dve.scalar_tensor_tensor(xf[f % 2], pair(J % 4), col(C_MAA + 1 + f), xx, ALU.add, ALU.mult).then_inc(s_mxd, 1)
                    dve.wait_ge(*read_count(b, idx))
                    dve.tensor_tensor(xf[f % 2], xf[f % 2], h, ALU.add).then_inc(s_xf, 1)

            def attn1_state(b):
                A = A1[b]
                hi, lo = h_hi[:, b * T:(b + 1) * T], h_lo[:, b * T:(b + 1) * T]
                dve.wait_ge(s_mxa, NACT * (b + 1))
                dve.scalar_tensor_tensor(yy, A["R"], col(C_U1), A["K"], ALU.mult, ALU.mult).then_inc(s_ruk, 1)
                dve.tensor_copy(hi, A["V"]).then_inc(s_vsp, 1)
                dve.wait_ge(s_vsp, 2 * b + 1)
                dve.tensor_tensor(lo, A["V"], hi.bitcast(F32), ALU.subtract).then_inc(s_vsp, 1)
                dve.wait_ge(s_q, b + 1)
                if b:
                    dve.wait_ge(s_out1, BPB * b)
                dve.tensor_tensor(y0, A["V"], pair(3), ALU.mult).then_inc(s_y0, 1)
                dve.wait_ge(s_dec, b + 1)

                def outer(j):
                    dve.wait_ge(s_vb, b * HK + j + 1)
                    dve.tensor_tensor(kv[j % 2], A["K"], pair(j % 2), ALU.mult).then_inc(s_kv, 1)

                def state(j):
                    n = b * HK + j
                    dve.wait_ge(s_kv, n + 1)
                    if n >= 2:
                        dve.wait_ge(s_prod, n - 1)
                    dve.tensor_tensor_scan(S[j % 2][:, 1:T + 1], A["dec"], kv[j % 2], 0.0, ALU.mult, ALU.add).then_inc(s_S, 1)

                outer(0)
                for j in range(HK):
                    if j + 1 < HK:
                        outer(j + 1)
                    state(j)
                dve.wait_ge(s_yps, HK * (b + 1))
                dve.wait_ge(s_y0, b + 1)
                dve.tensor_tensor(yy, y0, pair(2), ALU.add).then_inc(s_y, 1)
                dve.wait_ge(s_gm, b + 1)
                dve.tensor_tensor(y0, yy, pair(3), ALU.subtract).then_inc(s_gc, 1)
                dve.wait_ge(s_gd, b + 1)
                link(dve.reciprocal(yy, yy))
                link(dve.tensor_tensor(y0, y0, yy, ALU.mult))
                link(dve.tensor_scalar(y0, y0, col(C_LNG), col(C_LNB), ALU.mult, ALU.add))
                dve.tensor_tensor(y0, y0, A["G"], ALU.mult).then_inc(s_yn, 1)
                for i in range(BPB):
                    k = BPB * b + i
                    dve.wait_ge(s_out1, k + 1)
                    dve.scalar_tensor_tensor(blk(x, k), PP[:, i, :], gate[:, 1, 0, b:b + 1], blk(x, k),
                                             ALU.mult, ALU.add).then_inc(s_xup, 1)

            layer_norm(0)
            attn0()
            layer_norm(1)
            experts(0)
            layer_norm(2)
            for k in range(2):
                link(dve.memset(S[k][:, 0:1], 0.0))
            for b in range(NB):
                attn1_proj(b)
            for b in range(NB):
                attn1_state(b)
            layer_norm(3)
            experts(1)


def kernel(**inputs):
    import concourse.bacc as _bacc
    from concourse import mybir as _mybir
    from concourse.bass_utils import run_bass_kernel_spmd as _run

    I = {k: np.asarray(v) for k, v in inputs.items()}
    f32 = np.float32

    def column(a):
        return np.asarray(a).reshape(P, 1)

    cols = np.zeros((P, NCOL), f32)
    for c, name in ((C_TD0, "L0_attn_time_decay"), (C_U0, "L0_attn_time_first"), (C_MAA, "L1_attn_time_maa_x"),
                    (C_TD1, "L1_attn_time_decay"), (C_U1, "L1_attn_u"), (C_LNG, "L1_attn_ln_g"),
                    (C_LNB, "L1_attn_ln_b")):
        cols[:, c:c + 1] = column(I[name])
    for f, m in enumerate(MIXES):
        cols[:, C_MAA + 1 + f:C_MAA + 2 + f] = column(I["L1_attn_time_maa_" + m])
    cols[:, C_COND:C_COND + NB] = I["L0_c"].T
    cols[:, C_COND + NB:C_COND + 2 * NB] = I["L1_c"].T

    def expert_pack(w1, w2):
        w2 = w2.reshape(NE, NC, P, P).transpose(0, 2, 1, 3).reshape(NE, P, FH)
        return np.concatenate([w1, w2], axis=2)

    rows = np.arange(P)
    head, within = rows // HK, rows % HK
    same = (head[:, None] == head[None, :])
    consts = np.zeros((P, 19, P), f32)
    for j in range(HK):
        m = (same & (within == j)[:, None]).astype(f32)
        consts[:, j, :] = m
        consts[:, HK + j, :] = m.T
    consts[:, 16, :] = same
    consts[:, 17, :] = np.eye(P)
    consts[:, 18, :] = np.tile(np.arange(NE, 0, -1), NT)

    arrays = {
        "x_t": I["L0_attn_x"].reshape(N, P).T,
        "wrvk_t": I["L0_attn_W_rvk"].T,
        "wout0_t": I["L0_attn_W_out"].T,
        "cols": cols,
        "wmod": np.stack([I["L0_wmod"], I["L1_wmod"]], axis=1),
        "experts": np.concatenate([
            expert_pack(I["L0_ffn_W1"], I["L0_ffn_W2"]),
            expert_pack(I["L1_ffn_W1"].transpose(0, 2, 1), I["L1_ffn_W2"].transpose(0, 2, 1))], axis=0),
        "b1_t": I["L0_ffn_b1"].reshape(NE * NC, P).T,
        "b2": I["L0_ffn_b2"],
        "br": I["L0_ffn_br"],
        "wr": np.stack([I["L0_ffn_Wr"], I["L1_ffn_Wr"].T], axis=1),
        "maaw1": I["L1_attn_maa_w1"],
        "maaw2": I["L1_attn_maa_w2"].reshape(5 * EMIX, P),
        "tdw1": I["L1_attn_td_w1"],
        "tdw2": I["L1_attn_td_w2"],
        "wproj_t": np.stack([I["L1_attn_W" + n].T for n in "kvrgo"], axis=1),
        "consts": consts,
    }
    nc = _bacc.Bacc("TRN2", target_bir_lowering=False, num_devices=1)
    args, feed = [], {}
    for name, a in arrays.items():
        a = np.ascontiguousarray(a)
        feed[name + "_dram"] = a
        args.append(nc.dram_tensor(name + "_dram", a.shape, _mybir.dt.from_np(a.dtype), kind="ExternalInput").ap())
    args.append(nc.dram_tensor("out_t_dram", (P, N), F32, kind="ExternalOutput").ap())
    args.append(nc.dram_tensor("gates", (2, NE, N), F32, kind="Internal").ap())
    program(nc, *args)
    r = _run(nc, [feed], core_ids=[0])
    return np.ascontiguousarray(r.results[0]["out_t_dram"].T).reshape(NB, T, P)
```

```python
from contextlib import ExitStack

import numpy as np

import concourse.bass as bass
from concourse import mybir

F32 = mybir.dt.float32
F32R = mybir.dt.float32r
I32 = mybir.dt.int32
ALU = mybir.AluOpType
ACT = mybir.ActivationFunctionType
AX_X = mybir.AxisListType.X

P = 128
NB = 2
T = 1024
N = NB * T
BLK = 512
NBLK = N // BLK
BPB = T // BLK
NT = T // P
NE = 8
FH = 512
NC = FH // P
HALVES = 2 * NB
STEPS = BPB * NC
BODY = 2 * STEPS
BODIES = NE // 2
HALF = NE * STEPS
RING = 4
LOOK = 3
HK = 8
EMIX = 32
EDEC = 64
LN_EPS = 1e-5
GN_EPS = 1e-5 * 8 ** 2
NEG_BIG = -1e38
GATE_FLOOR = 0.25
ROOT_START = float(0x5F3759DF)

C_TD0, C_U0 = 0, 1
C_MAA = 2
C_TD1, C_U1, C_LNG, C_LNB = 8, 9, 10, 11
C_COND = 12
NCOL = 16

MIXES = ("w", "k", "v", "r", "g")
SLOTS = BPB * HK
KVR_PAIR = ((0, 1, 3), (2, 0, 1))
TABLE = ("gelu_and_others", "silu_and_others")
RECIP = 3
STEP_ACC = 8
T_OUT0, T_LN1, T_ROUTE1, T_START1 = 26, 32, 44, 59
T_LN2, T_PROJ, T_DEC, T_STATE0, T_G, T_GN0 = 3, 12, 23, 26, 47, 50
T_STATE1, T_GN, T_LN3, T_ROUTE3 = 6, 30, 42, 52
ST_BLOCK, ST_SPREAD, ST_OUTER, ST_GATHER, ST_TAKE = HK + 2, 2, 3, 5, HK + 6
SLOW, QUICK = (2, 4, 5, 6, 7, 8, 10), (-1, 0, 0, 1, 2, 3, 4)


def run(parts):
    for _ in parts:
        pass


def between(parts):
    due = [next(parts)]

    def after(step=float("inf")):
        while due[0] is not None and due[0] <= step:
            due[0] = next(parts, None)
    return after


def woven(*stages):
    due = [[next(parts), parts] for parts in stages]
    while due:
        first = min(due, key=lambda d: d[0])
        yield first[0]
        first[0] = next(first[1], None)
        if first[0] is None:
            due.remove(first)


def chained(stages):
    for parts in stages:
        yield from parts


def weave(*stages):
    run(woven(*stages))


def program(nc, x_d, wrvk_d, wout0_d, cols_d, wmod_d, wp_d, b1_d, b2_d, br_d, wr_d,
            maaw1_d, maaw2_d, tdw1_d, tdw2_d, wproj_d, const_d, out_d, gate_d):
    with ExitStack() as ctx:
        def sb(name, shape, dt=F32):
            return ctx.enter_context(nc.sbuf_tensor(name, shape, dt))

        def sem(name):
            return ctx.enter_context(nc.semaphore(name))

        x = sb("x", [P, N])
        H = sb("H", [P, NB, T + 1])
        h_hi = sb("h_hi", [P, N], F32R)
        h_lo = sb("h_lo", [P, N], F32R)
        w_hi = sb("w_hi", [P, 2, 2 * FH], F32R)
        w_lo = sb("w_lo", [P, 2, 2 * FH], F32R)
        w_raw = sb("w_raw", [P, 2, 2 * FH])
        g_hi = sb("g_hi", [P, RING, BLK], F32R)
        g_lo = sb("g_lo", [P, RING, BLK], F32R)
        sel = sb("sel", [P, HK, P], F32R)
        cols = sb("cols", [P, NCOL])
        wrvk = sb("wrvk", [P, 3 * P])
        wout0 = sb("wout0", [P, P])
        jmean = sb("jmean", [P, P])
        mod = sb("mod", [P, 2, 6, NB])
        gate_abs = sb("gate_abs", [P, 2, 2, NB])
        gate_sgn = sb("gate_sgn", [P, 2, 2, NB])
        cond = sb("cond", [P, 2 * NB])
        one_c = sb("one_c", [P, 2, 2, NB])
        gate = sb("gate", [P, 2, 2, NB])
        wdec = sb("wdec", [P, 1])
        b1 = sb("b1", [P, NE * NC])
        b1e = sb("b1e", [P, 2, NC])
        zero = sb("zero", [P, 1])
        b2 = sb("b2", [NE, P])
        br = sb("br", [P, NE])
        wr = sb("wr", [P, 2, NE])
        maaw1 = sb("maaw1", [P, 5 * EMIX])
        maaw2 = sb("maaw2", [P, P])
        maaw2g = sb("maaw2g", [EMIX, P])
        tdw1 = sb("tdw1", [P, EDEC])
        tdw2 = sb("tdw2", [EDEC, P])
        wproj = sb("wproj", [P, 5, P])
        consts = sb("consts", [P, 19, P])
        ident = consts[:, 17, :]
        headones = consts[:, 16, :]
        ranks = consts[:, 18, 0:NT * NE].rearrange("p (t e) -> p t e", e=NE)
        ones = sb("ones", [P, P])
        ln_rs = sb("ln_rs", [P, 3, BPB, BLK // P])
        gn_rs = sb("gn_rs", [P, 3, BPB, BLK // P, P // HK])
        headmean = sb("headmean", [P, P])
        carry = sb("carry", [P, HK])
        small = sb("small", [P, 12, NT])
        sm3 = sb("sm3", [P, 6, NT, NE])

        arena = sb("arena", [P, 26 * T + 8])
        at = [0]

        def blk(ap, i):
            return ap[:, i * BLK:(i + 1) * BLK]

        def view(width):
            a = arena[:, at[0]:at[0] + width]
            at[0] += width
            return a

        xc, sq = [None] * NB, [None] * NB
        xc[0], sq[0], xc[1], sq[1] = view(T), view(T), view(T), view(T)
        ln_end = at[0]
        A0 = []
        for b in range(NB):
            A0.append({k: view(T) for k in ("K", "V", "R", "p", "d1", "d2", "dE1", "dE2")}
                      | {k: view(T + 1) for k in ("pp", "aa", "bb")})
        at[0] = ln_end
        acc = view(N)
        gbc = view(2 * T).rearrange("p (r n) -> p r n", r=2)
        g32 = view(RING * BLK).rearrange("p (r n) -> p r n", r=RING)
        etmp = view(2 * BLK).rearrange("p (r n) -> p r n", r=2)
        g8 = view(T)
        gT = view(P)
        A1 = [{k: view(T) for k in ("K", "R", "V", "dec", "G")}]
        A1.append(A1[0] | {"G": xc[1]})
        y0, xx = [view(T), sq[1]], [view(T)]
        mixA, mixB, td1, xf = [view(T)], [view(T)], [view(T)], [[view(T), view(T)]]
        yy = [xx[0], xf[0][1]]
        kv = [blk(mixA[0], i) for i in range(2)]
        prod = [blk(mixB[0], 0), blk(mixB[0], 1), blk(td1[0], 0)]
        S = [view(BLK + 1), view(BLK + 1)]
        at[0] = ln_end
        xx.append(view(T))
        mixA.append(view(T))
        mixB.append(view(T))
        td1.append(view(T))
        xf.append([view(T), view(T)])
        PP = ctx.enter_context(nc.psum_tensor("PP", [P, 8, BLK], F32))

        def per_batch(name):
            return [sem(f"{name}{b}") for b in range(NB)]

        s_x = [sem(f"x_loaded{i}") for i in range(NBLK)]
        s_cols, s_small, s_mod_in = sem("cols_loaded"), sem("small_loaded"), sem("mod_loaded")
        s_a0w, s_a1w = sem("attn0_weights_loaded"), sem("attn1_weights_loaded")
        s_const, s_set = sem("consts_loaded"), sem("constants_set")
        s_silu, s_modps, s_mod = sem("cond_silu"), sem("mod_products"), sem("mod_ready")
        s_chain = sem("dve_chain")
        s_mean, s_xc, s_sq = per_batch("ln_mean"), per_batch("ln_centred"), per_batch("ln_squared")
        s_var, s_dg, s_rs = per_batch("ln_var"), per_batch("ln_inverse_on_diagonal"), per_batch("ln_inverse_spread")
        s_h, s_hsp = per_batch("ln_h"), sem("ln_h_split")
        s_xup = per_batch("x_updated")
        s_kvr = sem("attn0_products")
        s_ev0 = [sem("attn0_k_evacuated"), sem("attn0_v_evacuated"), sem("attn0_r_evacuated")]
        s_pp, s_arg, s_argp = sem("attn0_running_max"), sem("attn0_exp_args"), sem("attn0_pool_args")
        s_exp, s_e2v = sem("attn0_exps"), sem("attn0_weighted_values")
        s_den, s_ln, s_rden = sem("attn0_denominator"), sem("attn0_log"), sem("attn0_denominator_inverse")
        s_wkv, s_out0 = sem("attn0_wkv"), sem("attn0_out")
        s_logit, s_lev, s_lexp, s_gate = sem("logits"), sem("logits_shifted"), sem("logits_exp"), sem("gates_ready")
        s_gT, s_gTs, s_gdram = sem("gates_turned"), sem("gates_turned_copied"), sem("gates_in_dram")
        s_g8, s_gbc = sem("gates_rows_loaded"), [sem("gates_broadcast0"), sem("gates_broadcast1")]
        s_wraw, s_wsp, s_b1 = [sem("w_raw_loaded0"), sem("w_raw_loaded1")], sem("w_split"), sem("bias1_placed")
        s_p1, s_act, s_lo = sem("first_products"), sem("hidden_activated"), sem("hidden_low_part")
        s_p2, s_ev, s_bias2 = sem("second_products"), sem("expert_block_read"), sem("bias2_products")
        s_acc0, s_acc = sem("expert_sum_started"), sem("expert_sum")
        s_mx, s_mxa, s_mxd = sem("attn1_proj_products"), sem("attn1_act_read"), sem("attn1_dve_read")
        s_xmx, s_xf = sem("attn1_mixed_input"), sem("attn1_mix_ready")
        s_wexp, s_dec, s_G = sem("attn1_decay_rate"), sem("attn1_decay"), sem("attn1_output_gate")
        s_ruk, s_q, s_y0 = sem("attn1_ruk"), sem("attn1_q"), sem("attn1_y0")
        s_vsp, s_vb, s_kv = sem("attn1_v_split"), sem("attn1_v_spread"), sem("attn1_kv")
        s_S, s_prod, s_yps, s_y = sem("attn1_state"), sem("attn1_r_state"), sem("attn1_y_added"), sem("attn1_y")
        s_gm, s_gc, s_gs, s_gv = sem("gn_mean"), sem("gn_centred"), sem("gn_squared"), sem("gn_var")
        s_ge, s_gr = sem("gn_inverse_expanded"), sem("gn_inverse_spread")
        s_yn, s_out1, s_done = sem("attn1_gated"), sem("attn1_out"), sem("out_stored")

        def h_blk(i):
            b, o = i // BPB, (i % BPB) * BLK
            return H[:, b, 1 + o:1 + o + BLK]

        def ln_bank(l, b, i):
            return PP[:, (4 if (l, b) in ((0, 1), (2, 1)) else 6) + i, :]

        def side(i):
            return PP[:, 6 + i, :]

        def pair(i):
            return PP[:, 2 * i:2 * i + 2, :].rearrange("p a n -> p (a n)")

        block = ctx.enter_context(nc.Block())

        def job_bank(b, idx, i):
            return PP[:, (6 if b == 0 else 2 * (idx % 2)) + i, :]

        JOBS = [("mixA", "act"), ("mixB", "act"), ("Mw", "dve"), ("Mk", "dve"), ("td1", "act"), ("Mv", "dve"),
                ("k", "act"), ("td2", "act"), ("Mr", "dve"), ("v", "act"), ("Mg", "dve"), ("r", "act"), ("g", "act")]
        NACT = sum(r == "act" for _, r in JOBS)
        NDVE = len(JOBS) - NACT

        def read_count(b, idx, i):
            who = JOBS[idx][1]
            before = sum(r == who for _, r in JOBS[:idx])
            jobs = NACT if who == "act" else NDVE
            return (s_mxa if who == "act" else s_mxd), BPB * (jobs * b + before) + i + 1

        def job(name):
            return [n for n, _ in JOBS].index(name)

        ACC_HALF = BPB * NE

        @block.sync
        def _(sp):
            sp.dma_start(cols[:], cols_d).then_inc(s_cols, 16)
            for i in range(BPB):
                sp.dma_start(blk(x, i), blk(x_d, i)).then_inc(s_x[i], 16)
            sp.dma_start(H[:, :, 1:1 + 6 * P], wmod_d).then_inc(s_mod_in, 16)
            for i in range(BPB, NBLK):
                sp.dma_start(blk(x, i), blk(x_d, i)).then_inc(s_x[i], 16)
            sp.dma_start(wrvk[:], wrvk_d).then_inc(s_a0w, 16)
            sp.dma_start(wout0[:], wout0_d).then_inc(s_a0w, 16)
            sp.dma_start(b1[:], b1_d).then_inc(s_small, 16)
            sp.dma_start(b2[:], b2_d).then_inc(s_small, 16)
            sp.dma_start(br[:], br_d.partition_broadcast(P)).then_inc(s_small, 16)
            sp.dma_start(wr[:], wr_d).then_inc(s_small, 16)
            sp.dma_start(consts[:], const_d).then_inc(s_const, 16)
            sp.dma_start(w_raw[:, 0, :], wp_d[0]).then_inc(s_wraw[0], 16)
            sp.dma_start(w_raw[:, 1, :], wp_d[1]).then_inc(s_wraw[1], 16)
            sp.dma_start(maaw1[:], maaw1_d).then_inc(s_a1w, 16)
            sp.dma_start(maaw2[:], maaw2_d[0:P, :]).then_inc(s_a1w, 16)
            sp.dma_start(maaw2g[:], maaw2_d[P:P + EMIX, :]).then_inc(s_a1w, 16)
            sp.dma_start(tdw1[:], tdw1_d).then_inc(s_a1w, 16)
            sp.dma_start(tdw2[:], tdw2_d).then_inc(s_a1w, 16)
            sp.dma_start(wproj[:], wproj_d).then_inc(s_a1w, 16)

            def load_w(m, e, p):
                sp.wait_ge(s_wsp, 2 * (m - 1))
                sp.dma_start(w_raw[:, p, :], wp_d[bass.ds(e, 1)].rearrange("o p n -> p (o n)")
                             if not isinstance(e, int) else wp_d[e]).then_inc(s_wraw[p], 16)

            def load_g(h, e, p):
                m = NE * h + e
                if not (isinstance(m, int) and m < 2):
                    sp.wait_ge(s_ev, BPB * (m - 1))
                src = gate_d[h, bass.ds(e, 1), :] if not isinstance(e, int) else gate_d[h, e:e + 1, :]
                sp.dma_start(gbc[:, p, :], src.rearrange("o n -> (o n)").partition_broadcast(P)).then_inc(s_gbc[p], 16)

            for h in range(HALVES):
                sp.wait_ge(s_gTs, h + 1)
                sp.dma_start(gate_d[h].rearrange("e (t p) -> (e t) p", p=P), gT[0:NT * NE]).then_inc(s_gdram, 16)
                sp.wait_ge(s_gdram, 16 * (h + 1))
                if h == NB:
                    sp.wait_ge(s_mx, BPB * NB * len(JOBS))
                    sp.wait_ge(s_xf, BPB * NB * len(MIXES))
                if h < NB:
                    if h:
                        sp.wait_ge(s_acc0, BPB * h)
                    sp.dma_start(g8[0:NE, :], gate_d[h]).then_inc(s_g8, 16)
                load_g(h, 0, 0)
                load_g(h, 1, 1)
                first = NE * (h // NB)
                with sp.Fori(0, BODIES - 1) as i:
                    for p in range(2):
                        load_w(NE * h + 2 * i + 2 + p, first + 2 * i + 2 + p, p)
                        load_g(h, 2 * i + 2 + p, p)
                if h + 1 < HALVES:
                    for p in range(2):
                        load_w(NE * (h + 1) + p, NE * ((h + 1) // NB) + p, p)
            for i in range(NBLK):
                sp.wait_ge(s_xup[i // BPB], 3 * BPB + i % BPB + 1)
                sp.dma_start(blk(out_d, i), blk(x, i)).then_inc(s_done, 16)
            sp.wait_ge(s_done, 16 * NBLK)

        @block.gpsimd
        def _(pool):
            pool.memset(jmean[:], 1.0 / P).then_inc(s_set, 1)
            pool.memset(ones[:], 1.0).then_inc(s_set, 1)
            pool.memset(zero[:], 0.0).then_inc(s_set, 1)
            pool.memset(H[:, :, 0:1], 0.0).then_inc(s_set, 1)
            pool.wait_ge(s_const, 16)
            pool.tensor_copy(sel[:], consts[:, 0:HK, :]).then_inc(s_set, 1)
            pool.tensor_scalar(headmean[:], headones, 1.0 / HK, None, ALU.mult).then_inc(s_set, 1)

            pool.wait_ge(s_set, 6)

            def split_w(m, p, k, t=0):
                yield t
                pool.wait_ge(s_wraw[p], 16 * (k + 1))
                if not (isinstance(m, int) and m < 2):
                    pool.wait_ge(s_p2, STEPS * (m - 1))
                pool.tensor_tensor(w_hi[:, p, :], w_raw[:, p, :], zero[:, 0:1].broadcast_to([P, 2 * FH]), ALU.add).then_inc(s_wsp, 1)
                yield t + 3
                pool.wait_ge(s_wsp, 2 * m + 1)
                pool.tensor_tensor(w_lo[:, p, :], w_raw[:, p, :], w_hi[:, p, :].bitcast(F32), ALU.subtract).then_inc(s_wsp, 1)

            def split_ahead(h):
                for m in range(NE * h + 2, min(NE * (h + 1) + 2, NE * HALVES)):
                    yield from split_w(m, m % 2, m // 2, STEPS * (m - NE * h - 1))

            def states(b, t):
                for i in range(BPB):
                    for j in range(HK):
                        n = SLOTS * b + HK * i + j
                        yield t + ST_BLOCK * i + j + ST_OUTER + 1
                        pool.wait_ge(s_S, n + 1)
                        if n % SLOTS == 0:
                            pool.wait_ge(s_mx, BPB * len(JOBS) * (b + 1))
                        if n >= 3:
                            pool.wait_ge(s_yps, n - 2)
                        pool.tensor_tensor(prod[n % 3], blk(A1[b]["R"], i), S[n % 2][:, 0:BLK], ALU.mult).then_inc(s_prod, 1)

            def attn0_args(b):
                A = A0[b]
                pool.wait_ge(s_ev0[0], b + 1)
                pool.wait_ge(s_pp, b + 1)
                pool.tensor_tensor(A["dE2"], A["K"], A["pp"][:, 1:T + 1], ALU.subtract).then_inc(s_argp, 1)
                pool.wait_ge(s_arg, 3 * b + 2)
                pool.tensor_tensor(A["d1"], A["pp"][:, 0:T], A["p"], ALU.subtract).then_inc(s_argp, 1)

            def attn0_values(b):
                A = A0[b]
                pool.wait_ge(s_exp, 4 * b + 2)
                pool.wait_ge(s_ev0[1], b + 1)
                pool.wait_ge(s_arg, 3 * b + 3)
                pool.tensor_tensor(A["K"], A["dE2"], A["V"], ALU.mult).then_inc(s_e2v, 1)
                pool.wait_ge(s_exp, 4 * b + 4)
                pool.tensor_tensor(A["p"], A["d2"], A["V"], ALU.mult).then_inc(s_e2v, 1)

            for b in range(NB):
                attn0_args(b)
                attn0_values(b)
            run(split_w(0, 0, 0))
            run(split_w(1, 1, 0))
            with pool.Fori(0, BODIES) as i:
                for p in range(2):
                    run(split_w(2 * i + 2 + p, p, i + 1))
            weave(split_ahead(1), states(0, T_STATE0))
            weave(split_ahead(2), states(1, T_STATE1))
            with pool.Fori(0, BODIES - 1) as i:
                for p in range(2):
                    run(split_w(NE * 3 + 2 * i + 2 + p, p, BODIES * 3 + i + 1))

        @block.scalar
        def _(act):
            act.wait_ge(s_cols, 16)
            act.activation(cond[:], cols[:, C_COND:C_COND + 2 * NB], ACT.Silu).then_inc(s_silu, 1)
            act.activation(wdec[:], cols[:, C_TD0:C_TD0 + 1], ACT.Exp).then_inc(s_silu, 1)

            def layer_norm(l, b, t=0):
                k0 = BPB * l
                yield t + 2
                for i in range(BPB):
                    act.wait_ge(s_xc[b], k0 + i + 1)
                    act.activation(blk(sq[b], i), blk(xc[b], i), ACT.Square).then_inc(s_sq[b], 1)

            def attn0():
                def leave(b, n, func=ACT.Copy):
                    act.wait_ge(s_kvr, 3 * b + n + 1)
                    act.activation(A0[b]["KVR"[n]], pair(KVR_PAIR[b][n]), func).then_inc(s_ev0[n], 1)

                def exponentials(b):
                    A = A0[b]
                    for name, (count, value) in (("dE1", (s_arg, 3 * b + 1)), ("dE2", (s_argp, 2 * b + 1)),
                                                 ("d2", (s_arg, 3 * b + 3)), ("d1", (s_argp, 2 * b + 2))):
                        act.wait_ge(count, value)
                        act.activation(A[name], A[name], ACT.Exp).then_inc(s_exp, 1)

                act.preload_act_table_set("natural_log_exp_and_others")
                leave(0, 0)
                leave(0, 1)
                leave(1, 0)
                exponentials(0)
                leave(1, 1)
                d, first = A0[0]["pp"][:, 0:T], A0[0]["dE2"]
                act.wait_ge(s_den, 1)
                act.wait_ge(s_e2v, 1)
                act.activation(first, d, ACT.Ln).then_inc(s_ln, 1)
                act.wait_ge(s_ln, 1)
                act.activation(first, first, ACT.Exp, scale=-1.0).then_inc(s_rden, 1)
                act.preload_act_table_set("sigmoid_and_others")
                leave(0, 2, ACT.Sigmoid)
                leave(1, 2, ACT.Sigmoid)
                act.preload_act_table_set("natural_log_exp_and_others")
                exponentials(1)

            def route(h, t=0, alone=True):
                yield t + 3
                if alone:
                    act.preload_act_table_set("exp_and_others")
                act.wait_ge(s_lev, h + 1)
                act.activation(sm3[:, 1, :, :], sm3[:, 0, :, :], ACT.Exp).then_inc(s_lexp, 1)
                if alone:
                    act.preload_act_table_set(TABLE[h // NB])

            def experts(h, beside=None):
                F = h // NB

                def step(n, s, e):
                    act.wait_ge(s_p1, n + 1)
                    if not (isinstance(n, int) and n < RING):
                        act.wait_ge(s_p2, n - RING + 1)
                        act.wait_ge(s_lo, n - RING + 1)
                    kw = {}
                    if F == 0:
                        p = (s // STEPS) % 2
                        if s % STEPS == 0:
                            act.activation(b1e[:, p, :], b1[:, bass.ds(e * NC, NC)], ACT.Copy).then_inc(s_b1, 1)
                        act.wait_ge(s_b1, NE * h + e + 1)
                        kw = dict(bias=b1e[:, p, s % NC:s % NC + 1])
                    func = ACT.Gelu if F == 0 else ACT.Silu
                    act.activation(g32[:, s % RING, :], PP[:, s % RING, :], func, **kw).then_inc(s_act, 1)
                    act.activation(g_hi[:, s % RING, :], PP[:, s % RING, :], func, **kw).then_inc(s_act, 1)

                def body(i):
                    for s in range(BODY):
                        step(HALF * h + BODY * i + s, s, 2 * i + s // STEPS)
                        if beside:
                            beside(BODY * i + s)

                if h == NB:
                    act.wait_ge(s_mx, BPB * NB * len(JOBS))
                if beside:
                    for i in range(BODIES):
                        body(i)
                    beside()
                else:
                    with act.Fori(0, BODIES) as i:
                        body(i)

            def attn1_proj(b, t, every):
                for idx, (name, reader) in enumerate(JOBS):
                    yield t + every * idx + 1
                    if reader != "act":
                        continue
                    for i in range(BPB):
                        src = job_bank(b, idx, i)
                        act.wait_ge(s_mx, BPB * (len(JOBS) * b + idx) + i + 1)
                        if name == "mixA":
                            act.activation(blk(mixA[b], i), src, ACT.Tanh).then_inc(s_mxa, 1)
                        elif name == "mixB":
                            act.activation(blk(mixB[b], i)[0:EMIX], src[0:EMIX], ACT.Tanh).then_inc(s_mxa, 1)
                        elif name == "td1":
                            act.activation(blk(td1[b], i)[0:EDEC], src[0:EDEC], ACT.Tanh).then_inc(s_mxa, 1)
                        elif name == "td2":
                            act.activation(blk(A1[b]["dec"], i), src, ACT.Copy).then_inc(s_mxa, 1)
                        elif name == "g":
                            act.activation(blk(A1[b]["G"], i), src, ACT.Copy).then_inc(s_mxa, 1)
                        else:
                            act.activation(blk(A1[b][name.upper()], i), src, ACT.Copy).then_inc(s_mxa, 1)

            def decay(b, t=0, table=None):
                yield t
                if table:
                    act.preload_act_table_set("exp_and_others")
                for i in range(BPB):
                    at = blk(A1[b]["dec"], i)
                    act.wait_ge(*read_count(b, job("td2"), i))
                    act.activation(at, at, ACT.Exp, bias=cols[:, C_TD1:C_TD1 + 1]).then_inc(s_wexp, 1)
                for i in range(BPB):
                    at = blk(A1[b]["dec"], i)
                    act.wait_ge(s_wexp, BPB * b + i + 1)
                    act.activation(at, at, ACT.Exp, scale=-1.0).then_inc(s_dec, 1)
                if table:
                    act.preload_act_table_set(table)

            def output_gate(b, t=0, table=None):
                yield t
                if table:
                    act.preload_act_table_set(TABLE[1])
                for i in range(BPB):
                    act.wait_ge(*read_count(b, job("g"), i))
                    act.activation(blk(A1[b]["G"], i), blk(A1[b]["G"], i), ACT.Silu).then_inc(s_G, 1)
                if table:
                    act.preload_act_table_set(table)

            def group_norm(b, t=0):
                yield t + 2
                for i in range(BPB):
                    act.wait_ge(s_gc, BPB * b + i + 1)
                    act.activation(blk(yy[b], i), blk(y0[b], i), ACT.Square).then_inc(s_gs, 1)

            for b in range(NB):
                run(layer_norm(0, b))
            attn0()
            run(layer_norm(1, 0))
            run(route(0))

            def rest0():
                yield from layer_norm(1, 1, T_LN1)
                yield from route(1, T_ROUTE1)

            experts(0, between(rest0()))

            def start1():
                yield from layer_norm(2, 0, T_LN2)
                yield from attn1_proj(0, T_PROJ, 1)

            def tables0():
                yield from decay(0, T_DEC, TABLE[0])
                yield from output_gate(0, T_G, TABLE[0])

            def chain0():
                yield from start1()
                yield from group_norm(0, T_GN0)

            experts(1, between(woven(chain0(), tables0())))

            def join1():
                yield from layer_norm(2, 1)
                yield from attn1_proj(1, 9, 1)

            def normed0():
                yield from layer_norm(3, 0)
                yield from route(2, 13, alone=False)

            act.preload_act_table_set("exp_and_others")
            weave(join1(), normed0(), decay(1, 20))
            act.preload_act_table_set(TABLE[1])

            def rest1():
                yield from output_gate(1, 2)
                yield from group_norm(1, T_GN)
                yield from layer_norm(3, 1, T_LN3)
                yield from route(3, T_ROUTE3)

            experts(2, between(rest1()))
            experts(3)

        @block.tensor
        def _(pe):
            def modulation():
                yield 1
                pe.wait_ge(s_silu, 1)
                pe.wait_ge(s_mod_in, 16)
                for l in range(2):
                    for j in range(6):
                        at0 = (l * 6 + j) * NB
                        last = pe.matmul(PP[:, 0, at0:at0 + NB], H[:, l, 1 + j * P:1 + (j + 1) * P],
                                         cond[:, l * NB:(l + 1) * NB], start=True, stop=True)
                last.then_inc(s_modps, 1)

            def layer_norm(l, b, t=0):
                k0 = BPB * l
                yield t
                for i in range(BPB):
                    if l == 0:
                        pe.wait_ge(s_x[BPB * b + i], 16)
                        pe.wait_ge(s_set, 2)
                    else:
                        pe.wait_ge(s_xup[b], k0 - BPB + i + 1)
                    pe.matmul(ln_bank(l, b, i), jmean[:], blk(x, BPB * b + i), start=True, stop=True).then_inc(s_mean[b], 1)
                yield t + 3
                for i in range(BPB):
                    pe.wait_ge(s_sq[b], k0 + i + 1)
                    for n in range(BLK // P):
                        last = pe.matmul(ln_bank(l, b, i)[:, n:n + 1], blk(sq[b], i)[:, n * P:(n + 1) * P],
                                         jmean[:, 0:1], start=True, stop=True)
                    last.then_inc(s_var[b], 1)
                yield t + 6
                for i in range(BPB):
                    pe.wait_ge(s_dg[b], k0 + i + 1)
                    pe.matmul(ln_bank(l, b, i), ones[:], blk(sq[b], i), start=True, stop=True).then_inc(s_rs[b], 1)

            def attn0(b, t=0):
                yield t
                pe.wait_ge(s_a0w, 32)
                pe.wait_ge(s_mod, 1)
                pe.wait_ge(s_h[b], BPB)
                for n, at0 in enumerate((2 * P, P, 0)):
                    if b and n:
                        pe.wait_ge(s_ev0[n - 1], 1)
                    for i in range(BPB):
                        last = pe.matmul(PP[:, 2 * KVR_PAIR[b][n] + i, :], wrvk[:, at0:at0 + P],
                                         h_blk(BPB * b + i), start=True, stop=True)
                    last.then_inc(s_kvr, 1)

            def attn0_out(b, t=0):
                yield t
                pe.wait_ge(s_wkv, b + 1)
                if b == 0:
                    pe.wait_ge(s_ev0[2], 1)
                else:
                    pe.wait_ge(s_gTs, 1)
                for i in range(BPB):
                    pe.matmul(side(i), wout0[:], blk(A0[b]["p"], i), start=True, stop=True).then_inc(s_out0, 1)

            def route(h, t=0, turn=8):
                F, b = h // NB, h % NB
                yield t
                pe.wait_ge(s_h[b], BPB * (2 * F + 2))
                pe.wait_ge(s_small, 16 * 4)
                for n in range(NT):
                    last = pe.matmul(PP[:, 6, n * NE:(n + 1) * NE], H[:, b, 1 + n * P:1 + (n + 1) * P], wr[:, F, :],
                                     start=True, stop=True)
                last.then_inc(s_logit, 1)
                yield t + turn
                pe.wait_ge(s_gate, h + 1)
                pe.wait_ge(s_const, 16)
                pe.transpose(PP[0:NT * NE, 7, 0:P], sm3[:, 5, :, :].rearrange("p t e -> p (t e)"), ident).then_inc(s_gT, 1)

            def stage1(h, i, s):
                if isinstance(i, int) and i == BODIES - 1 and s >= BODY:
                    h, i, s = h + 1, 0, s - BODY
                F, b = h // NB, h % NB
                m0 = NE * h + 2 * i
                p, st = (s // STEPS) % 2, s % STEPS
                k, c = BPB * b + st // NC, st % NC
                n = m0 * STEPS + s
                if st == 0:
                    pe.wait_ge(s_wsp, 2 * (m0 + s // STEPS + 1))
                if c == 0:
                    pe.wait_ge(s_hsp, 2 * (NBLK * F + k + 1))
                if not (isinstance(n, int) and n < RING):
                    pe.wait_ge(s_act, 2 * (n - RING + 1))
                w = slice(c * P, (c + 1) * P)
                ps = PP[:, s % RING, :]
                pe.matmul(ps, w_lo[:, p, w], blk(h_hi, k), start=True, stop=False)
                pe.matmul(ps, w_hi[:, p, w], blk(h_lo, k), start=False, stop=False)
                pe.matmul(ps, w_hi[:, p, w], blk(h_hi, k), start=False, stop=True).then_inc(s_p1, 1)

            def stage2(h, i, s):
                m0 = NE * h + 2 * i
                p, st = (s // STEPS) % 2, s % STEPS
                c, q = st % NC, s // NC
                n = m0 * STEPS + s
                if c == 0 and not (isinstance(n, int) and n < 2 * NC):
                    pe.wait_ge(s_ev, m0 * BPB + q - 1)
                pe.wait_ge(s_act, 2 * (n + 1))
                pe.wait_ge(s_lo, n + 1)
                w = slice(FH + c * P, FH + (c + 1) * P)
                ps = PP[:, 4 + q % 2, :]
                pe.matmul(ps, w_lo[:, p, w], g_hi[:, s % RING, :], start=(c == 0), stop=False)
                pe.matmul(ps, w_hi[:, p, w], g_lo[:, s % RING, :], start=False, stop=False)
                pe.matmul(ps, w_hi[:, p, w], g_hi[:, s % RING, :], start=False, stop=(c == NC - 1)).then_inc(s_p2, 1)

            def start_sum(h, t):
                yield t
                pe.wait_ge(s_g8, 16 * (h + 1))
                for k in range(BPB):
                    pe.matmul(side(k), b2[:], blk(g8, k)[0:NE], start=True, stop=True).then_inc(s_bias2, 1)

            def experts(h, beside=None, joined=False):
                def body(i, last=False):
                    for s in range(BODY):
                        if not (last and s + LOOK >= BODY):
                            stage1(h, i, s + LOOK)
                        stage2(h, i, s)
                        if beside:
                            beside(BODY * i + s)

                if beside:
                    for i in range(BODIES):
                        body(i, last=i == BODIES - 1 and not joined)
                    beside()
                else:
                    with pe.Fori(0, BODIES - 1) as i:
                        body(i)
                    body(BODIES - 1, last=not joined)

            def attn1_proj(b, t, every):
                for idx, (name, reader) in enumerate(JOBS):
                    yield t + every * idx
                    for i in range(BPB):
                        if idx > b:
                            pe.wait_ge(*read_count(b, idx - 1 - b, i))
                        rows = P
                        if name in ("mixA", "mixB"):
                            pe.wait_ge(s_xmx, BPB * b + i + 1)
                            lhs, rows = (maaw1[:, 0:P], P) if name == "mixA" else (maaw1[:, P:5 * EMIX], EMIX)
                            src = y0[b]
                        elif name[0] == "M":
                            f = MIXES.index(name[1])
                            if f < 4:
                                pe.wait_ge(*read_count(b, 0, i))
                                lhs, src = maaw2[f * EMIX:(f + 1) * EMIX, :], mixA[b][f * EMIX:(f + 1) * EMIX]
                            else:
                                pe.wait_ge(*read_count(b, 1, i))
                                lhs, src = maaw2g[:], mixB[b][0:EMIX]
                        elif name == "td1":
                            pe.wait_ge(s_xf, BPB * 5 * b + i + 1)
                            lhs, src, rows = tdw1[:], xf[b][0], EDEC
                        elif name == "td2":
                            pe.wait_ge(*read_count(b, job("td1"), i))
                            lhs, src = tdw2[:], td1[b][0:EDEC]
                        else:
                            f = MIXES.index(name)
                            pe.wait_ge(s_xf, BPB * (5 * b + f) + i + 1)
                            lhs, src = wproj[:, {"k": 0, "v": 1, "r": 2, "g": 3}[name], :], xf[b][f % 2]
                        pe.matmul(job_bank(b, idx, i)[0:rows], lhs, blk(src, i), start=True, stop=True).then_inc(s_mx, 1)

            def attn1_state(b, t):
                def bonus(i):
                    pe.wait_ge(s_ruk, BPB * b + i + 1)
                    if i:
                        pe.wait_ge(s_kv, SLOTS * b + HK * i)
                    pe.matmul(side(0), headones, blk(yy[b], i), start=True, stop=True).then_inc(s_q, 1)

                def spread(i, j):
                    n = SLOTS * b + HK * i + j
                    if j:
                        pe.wait_ge(s_kv, n)
                    else:
                        pe.wait_ge(s_vsp, 2 * (b + 1))
                        pe.wait_ge(s_y0, BPB * b + i + 1)
                    pe.matmul(side(0), sel[:, j, :], blk(h_lo, BPB * b + i), start=True, stop=False)
                    pe.matmul(side(0), sel[:, j, :], blk(h_hi, BPB * b + i), start=False, stop=True).then_inc(s_vb, 1)

                def gather(i, j):
                    n = SLOTS * b + HK * i + j
                    pe.wait_ge(s_prod, n + 1)
                    if i and j == 0:
                        pe.wait_ge(s_y, BPB * b + i)
                    pe.matmul(side(1), consts[:, HK + j, :], prod[n % 3], start=(j == 0), stop=(j == HK - 1),
                              skip_group_check=True).then_inc(s_yps, 1)

                def inputs(i):
                    yield t + ST_BLOCK * i
                    bonus(i)
                    for j in range(HK):
                        yield t + ST_BLOCK * i + ST_SPREAD + j
                        spread(i, j)

                def sums(i):
                    for j in range(HK):
                        yield t + ST_BLOCK * i + ST_GATHER + j
                        gather(i, j)

                yield t
                pe.wait_ge(s_mxa, BPB * NACT * (b + 1))
                if b:
                    pe.wait_ge(s_gTs, NB + 1)
                yield from woven(chained(inputs(i) for i in range(BPB)), chained(sums(i) for i in range(BPB)))

            def group_norm(b, t=0):
                heads = P // HK
                yield t
                for i in range(BPB):
                    pe.wait_ge(s_kv, SLOTS * (b + 1))
                    pe.wait_ge(s_y, BPB * (b + 1))
                    pe.matmul(side(i), headmean[:], blk(yy[b], i), start=True, stop=True).then_inc(s_gm, 1)
                yield t + 3
                for i in range(BPB):
                    pe.wait_ge(s_gs, BPB * b + i + 1)
                    for n in range(BLK // P):
                        last = pe.matmul(side(i)[:, n * heads:(n + 1) * heads], blk(yy[b], i)[:, n * P:(n + 1) * P],
                                         headmean[:, 0:P:HK], start=True, stop=True)
                    last.then_inc(s_gv, 1)
                yield t + 6
                for i in range(BPB):
                    pe.wait_ge(s_ge, BPB * b + i + 1)
                    for n in range(BLK // P):
                        last = pe.matmul(side(i)[:, n * P:(n + 1) * P], blk(yy[b], i)[:, n * P:(n + 1) * P], ident,
                                         start=True, stop=True)
                    last.then_inc(s_gr, 1)
                yield t + 9
                for i in range(BPB):
                    pe.wait_ge(s_yn, BPB * b + i + 1)
                    pe.matmul(side(i), wproj[:, 4, :], blk(y0[b], i), start=True, stop=True).then_inc(s_out1, 1)

            def first0():
                yield from layer_norm(0, 0)
                yield from attn0(0, 12)

            def first1():
                yield from layer_norm(0, 1, 3)
                yield from attn0(1, 16)

            weave(first0(), modulation(), first1())
            run(attn0_out(0))
            run(layer_norm(1, 0))

            def rest0():
                yield from route(0, -1, 4)
                yield from start_sum(0, STEP_ACC)
                yield from attn0_out(1, T_OUT0)
                yield from layer_norm(1, 1, T_LN1)
                yield from route(1, T_ROUTE1)
                yield from start_sum(1, T_START1)

            beside = between(rest0())
            beside(-1)
            for s in range(LOOK):
                stage1(0, 0, s)
            experts(0, beside, joined=True)

            def start1():
                yield T_LN2
                pe.wait_ge(s_a1w, 16 * 6)
                pe.wait_ge(s_set, 6)
                yield from layer_norm(2, 0, T_LN2)
                yield from attn1_proj(0, T_PROJ, 1)
                yield from attn1_state(0, T_STATE0)
                yield from group_norm(0, T_GN0)

            experts(1, between(start1()))

            def join1():
                yield from layer_norm(2, 1)
                yield from attn1_proj(1, 9, 1)

            def normed0():
                yield from layer_norm(3, 0)
                yield from route(2, 13)

            weave(join1(), normed0())

            def rest1():
                yield from attn1_state(1, T_STATE1)
                yield from group_norm(1, T_GN)
                yield from layer_norm(3, 1, T_LN3)
                yield from route(3, T_ROUTE3)

            pe.wait_ge(s_mxa, BPB * NB * NACT)
            pe.wait_ge(s_mxd, BPB * NB * NDVE)
            for s in range(LOOK):
                stage1(NB, 0, s)
            experts(2, between(rest1()), joined=True)
            experts(3)

        @block.vector
        def _(dve):
            chain = [0]

            def link(ins):
                chain[0] += 1
                ins.then_inc(s_chain, 1)
                dve.wait_ge(s_chain, chain[0])

            def col(c):
                return cols[:, c:c + 1]

            def modulation():
                yield 2
                dve.wait_ge(s_modps, 1)
                link(dve.tensor_copy(mod[:].rearrange("p l j b -> p (l j b)"), PP[:, 0, 0:2 * 6 * NB]))
                for l in range(2):
                    sc, ga = mod[:, l, 1:6:3, :], mod[:, l, 2:6:3, :]
                    dve.tensor_scalar(one_c[:, l], sc, 1.0, None, ALU.add).then_inc(s_mod, 1)
                    link(dve.tensor_scalar(gate_sgn[:, l], ga, 0.0, 2.0, ALU.is_ge, ALU.mult))
                    link(dve.tensor_scalar(gate_sgn[:, l], gate_sgn[:, l], -1.0, None, ALU.add))
                    link(dve.tensor_tensor(gate_abs[:, l], gate_sgn[:, l], ga, ALU.mult))
                    dve.scalar_tensor_tensor(gate[:, l], gate_abs[:, l], GATE_FLOOR, gate_sgn[:, l], ALU.max,
                                             ALU.mult).then_inc(s_mod, 1)
                dve.wait_ge(s_silu, 2)
                link(dve.tensor_scalar(wdec[:], wdec[:], -1.0, None, ALU.mult))
                dve.wait_ge(s_mod, 4)
                dve.wait_ge(s_const, 16)

            def inverse_root(at):
                v, y, w = at
                link(dve.tensor_scalar(y.bitcast(I32), v.bitcast(I32), -0.5, ROOT_START, ALU.mult, ALU.add))
                for _ in range(3):
                    link(dve.scalar_tensor_tensor(w, y, -0.5, v, ALU.mult, ALU.mult))
                    link(dve.tensor_tensor(w, w, y, ALU.mult))
                    link(dve.scalar_tensor_tensor(y, w, 1.5, y, ALU.add, ALU.mult))

            def layer_norm(l, b, t=0):
                half, L = l % 2, l // 2
                k0 = BPB * l
                yield t + 2
                for i in range(BPB):
                    dve.wait_ge(s_mean[b], k0 + i + 1)
                    dve.tensor_tensor(blk(xc[b], i), blk(x, BPB * b + i), ln_bank(l, b, i), ALU.subtract).then_inc(s_xc[b], 1)
                yield t + 5
                for i in range(BPB):
                    dve.wait_ge(s_var[b], k0 + i + 1)
                    link(dve.tensor_scalar(ln_rs[:, 0, i, :], ln_bank(l, b, i)[:, 0:BLK // P], LN_EPS, None, ALU.add))
                inverse_root([ln_rs[:, n].rearrange("p k t -> p (k t)") for n in range(3)])
                for i in range(BPB):
                    dve.tensor_tensor(blk(sq[b], i).rearrange("p (t n) -> p t n", n=P),
                                      ident.unsqueeze(1).broadcast_to([P, BLK // P, P]),
                                      ln_rs[:, 1, i, :].unsqueeze(2).broadcast_to([P, BLK // P, P]),
                                      ALU.mult).then_inc(s_dg[b], 1)
                for i in range(BPB):
                    yield t + 8 + i
                    k = BPB * b + i
                    dve.wait_ge(s_rs[b], k0 + i + 1)
                    link(dve.scalar_tensor_tensor(blk(xc[b], i), blk(xc[b], i), one_c[:, L, half, b:b + 1],
                                                  ln_bank(l, b, i), ALU.mult, ALU.mult))
                    dve.tensor_scalar(h_blk(k), blk(xc[b], i), mod[:, L, 3 * half, b:b + 1], None, ALU.add).then_inc(s_h[b], 1)
                    if half:
                        yield t + 8 + i
                        dve.wait_ge(s_h[b], k0 + i + 1)
                        dve.tensor_copy(blk(h_hi, k), h_blk(k)).then_inc(s_hsp, 1)
                        dve.wait_ge(s_hsp, 2 * (NBLK * L + k) + 1)
                        dve.tensor_tensor(blk(h_lo, k), h_blk(k), blk(h_hi, k).bitcast(F32), ALU.subtract).then_inc(s_hsp, 1)

            def attn0_exponents(b):
                A = A0[b]
                yield
                dve.memset(A["pp"][:, 0:1], NEG_BIG)
                dve.memset(A["aa"][:, 0:1], 0.0)
                link(dve.memset(A["bb"][:, 0:1], 0.0))
                prev = A["pp"][:, 0:T]
                dve.wait_ge(s_ev0[0], b + 1)
                dve.tensor_tensor_scan(A["pp"][:, 1:T + 1], wdec[:, 0:1].broadcast_to([P, T]), A["K"], NEG_BIG,
                                       ALU.add, ALU.max).then_inc(s_pp, 1)
                dve.wait_ge(s_pp, b + 1)
                dve.scalar_tensor_tensor(A["dE1"], prev, wdec[:, 0:1], A["pp"][:, 1:T + 1], ALU.add,
                                         ALU.subtract).then_inc(s_arg, 1)
                yield
                dve.scalar_tensor_tensor(A["p"], A["K"], col(C_U0), prev, ALU.add, ALU.max).then_inc(s_arg, 1)
                dve.wait_ge(s_arg, 3 * b + 2)
                dve.scalar_tensor_tensor(A["d2"], A["K"], col(C_U0), A["p"], ALU.add, ALU.subtract).then_inc(s_arg, 1)

            def attn0_denominator(b, t=0):
                A = A0[b]
                yield t
                dve.wait_ge(s_exp, 4 * b + 2)
                link(dve.tensor_tensor_scan(A["bb"][:, 1:T + 1], A["dE1"], A["dE2"], 0.0, ALU.mult, ALU.add))
                yield t + 3
                den = A["pp"][:, 0:T]
                dve.wait_ge(s_exp, 4 * b + 4)
                link(dve.tensor_tensor(den, A["d1"], A["bb"][:, 0:T], ALU.mult))
                dve.tensor_tensor(den, den, A["d2"], ALU.add).then_inc(s_den, 1)
                yield t + 5
                dve.wait_ge(s_e2v, 2 * b + 1)
                link(dve.tensor_tensor_scan(A["aa"][:, 1:T + 1], A["dE1"], A["K"], 0.0, ALU.mult, ALU.add))

            def attn0_numerator(b, t=0):
                A = A0[b]
                yield t
                link(dve.tensor_tensor(A["d1"], A["d1"], A["aa"][:, 0:T], ALU.mult))
                yield t + 1
                dve.wait_ge(s_e2v, 2 * b + 2)
                link(dve.tensor_tensor(A["d1"], A["d1"], A["p"], ALU.add))

            def attn0_quotient0():
                A = A0[0]
                dve.wait_ge(s_rden, 1)
                dve.wait_ge(s_ev0[2], 1)
                den = A["pp"][:, 0:T]
                link(dve.tensor_tensor(den, den, A["dE2"], ALU.mult))
                link(dve.scalar_tensor_tensor(den, den, -2.0, A["dE2"], ALU.add, ALU.mult))
                link(dve.tensor_tensor(A["d1"], A["d1"], den, ALU.mult))
                dve.scalar_tensor_tensor(A["p"], A["d1"], -1.0, A["R"], ALU.mult, ALU.mult).then_inc(s_wkv, 1)

            def attn0_quotient1(t):
                A = A0[1]
                den = A["pp"][:, 0:T]
                dve.wait_ge(s_den, 2)
                for c in range(4):
                    yield t + RECIP * c
                    part = slice(c * T // 4, (c + 1) * T // 4)
                    link(dve.reciprocal(den[:, part], den[:, part]))
                yield t + 4 * RECIP
                link(dve.tensor_tensor(A["d1"], A["d1"], den, ALU.mult))
                yield t + 4 * RECIP + 1
                dve.wait_ge(s_ev0[2], 2)
                dve.tensor_tensor(A["p"], A["d1"], A["R"], ALU.mult).then_inc(s_wkv, 1)

            def attn0_add(b, t=0):
                yield t
                for i in range(BPB):
                    k = BPB * b + i
                    dve.wait_ge(s_out0, k + 1)
                    dve.scalar_tensor_tensor(blk(x, k), side(i), gate[:, 0, 0, b:b + 1], blk(x, k),
                                             ALU.mult, ALU.add).then_inc(s_xup[b], 1)

            def over_experts(k):
                return small[:, k, :].unsqueeze(2).broadcast_to([P, NT, NE])

            def route(h, steps):
                F = h // NB
                logits = PP[:, 6, 0:NT * NE].rearrange("p (t e) -> p t e", e=NE)
                yield steps[0]
                dve.wait_ge(s_logit, h + 1)
                if F == 0:
                    link(dve.tensor_tensor(sm3[:, 0], logits, br[:].unsqueeze(1).broadcast_to([P, NT, NE]), ALU.add))
                else:
                    link(dve.tensor_copy(sm3[:, 0], logits))
                link(dve.tensor_reduce(small[:, 0, :], sm3[:, 0], AX_X, ALU.max))
                dve.tensor_tensor(sm3[:, 0], sm3[:, 0], over_experts(0), ALU.subtract).then_inc(s_lev, 1)
                yield steps[1]
                dve.wait_ge(s_lexp, h + 1)
                link(dve.tensor_reduce(small[:, 1, :], sm3[:, 1], AX_X, ALU.add))
                link(dve.reciprocal(small[:, 2, :], small[:, 1, :]))
                link(dve.tensor_tensor(sm3[:, 0], sm3[:, 1], over_experts(2), ALU.mult))

                def pick(k, onehot):
                    link(dve.tensor_reduce(small[:, k, :], sm3[:, 0], AX_X, ALU.max))
                    link(dve.tensor_tensor(sm3[:, 2], sm3[:, 0], over_experts(k), ALU.is_equal))
                    link(dve.tensor_tensor(sm3[:, 2], sm3[:, 2], ranks, ALU.mult))
                    link(dve.tensor_reduce(small[:, k + 1, :], sm3[:, 2], AX_X, ALU.max))
                    link(dve.tensor_tensor(sm3[:, onehot], sm3[:, 2], over_experts(k + 1), ALU.is_equal))

                dve.wait_ge(s_const, 16)
                yield steps[2]
                pick(3, 3)
                yield steps[3]
                link(dve.scalar_tensor_tensor(sm3[:, 0], sm3[:, 3], -2.0, sm3[:, 0], ALU.mult, ALU.add))
                pick(5, 4)
                yield steps[4]
                link(dve.tensor_tensor(small[:, 7, :], small[:, 3, :], small[:, 5, :], ALU.add))
                link(dve.reciprocal(small[:, 8, :], small[:, 7, :]))
                link(dve.tensor_tensor(small[:, 9, :], small[:, 3, :], small[:, 8, :], ALU.mult))
                link(dve.tensor_tensor(small[:, 10, :], small[:, 5, :], small[:, 8, :], ALU.mult))
                yield steps[5]
                link(dve.tensor_tensor(sm3[:, 3], sm3[:, 3], over_experts(9), ALU.mult))
                link(dve.tensor_tensor(sm3[:, 4], sm3[:, 4], over_experts(10), ALU.mult))
                gout = sm3[:, 5].rearrange("p t e -> p (t e)").rearrange("p (e t) -> p t e", t=NT)
                dve.tensor_tensor(gout, sm3[:, 3], sm3[:, 4], ALU.add).then_inc(s_gate, 1)
                yield steps[6]
                dve.wait_ge(s_gT, h + 1)
                if h:
                    dve.wait_ge(s_gdram, 16 * h)
                dve.tensor_copy(gT[0:NT * NE], PP[0:NT * NE, 7, 0:P]).then_inc(s_gTs, 1)

            def low(n, s):
                dve.wait_ge(s_act, 2 * (n + 1))
                if not (isinstance(n, int) and n < RING):
                    dve.wait_ge(s_p2, n - RING + 1)
                dve.tensor_tensor(g_lo[:, s % RING, :], g32[:, s % RING, :], g_hi[:, s % RING, :].bitcast(F32),
                                  ALU.subtract).then_inc(s_lo, 1)

            def read_block(h, i, r):
                q = BPB * (NE * h + 2 * i) + r
                p = (r // BPB) % 2
                dve.wait_ge(s_p2, NC * (q + 1))
                if r % BPB == 0:
                    dve.wait_ge(s_gbc[p], 16 * (BODIES * h + i + 1 + (r // BPB) // 2))
                dve.tensor_tensor(etmp[:, r % 2, :], PP[:, 4 + r % 2, :], blk(gbc[:, p, :], r % BPB), ALU.mult).then_inc(s_ev, 1)

            def add_block(h, i, r):
                q = BPB * 2 * i + r
                at = blk(acc, BPB * (h % NB) + r % BPB)
                dve.wait_ge(s_ev, BPB * NE * h + q + 1)
                if isinstance(q, int) and q < BPB:
                    dve.wait_ge(s_acc0, BPB * h + q + 1)
                else:
                    dve.wait_ge(s_acc, ACC_HALF * h + q - BPB + 1)
                dve.tensor_tensor(at, at, etmp[:, r % 2, :], ALU.add).then_inc(s_acc, 1)

            def start_sum(h, t):
                yield t
                for k in range(BPB):
                    at = blk(acc, BPB * (h % NB) + k)
                    if h < NB:
                        dve.wait_ge(s_bias2, BPB * h + k + 1)
                        dve.tensor_copy(at, side(k)).then_inc(s_acc0, 1)
                    else:
                        dve.memset(at, 0.0).then_inc(s_acc0, 1)

            def finish(h):
                F, b = h // NB, h % NB
                read_block(h, BODIES, -1)
                add_block(h, BODIES, -1)
                yield
                for k in range(BPB * b, BPB * (b + 1)):
                    dve.wait_ge(s_acc, ACC_HALF * (h + 1) - BPB + k % BPB + 1)
                    dve.scalar_tensor_tensor(blk(x, k), blk(acc, k), gate[:, F, 1, b:b + 1], blk(x, k),
                                             ALU.mult, ALU.add).then_inc(s_xup[b], 1)

            def experts(h, beside=None, before=None):
                def body(i):
                    for s in range(BODY):
                        low(HALF * h + BODY * i + s, s)
                        first = isinstance(i, int) and i == 0
                        late = first and h == 0
                        if first and s in (1, 3):
                            if before:
                                next(before, None)
                        elif s % NC == 1 and not (late and s == 5):
                            read_block(h, i, s // NC - 1)
                        if late and s == 7:
                            read_block(h, i, 0)
                        if late and s == 9:
                            add_block(h, i, 0)
                        elif s % NC == 2 and not (first and s == 2) and not (late and s == 6):
                            add_block(h, i, s // NC - 1)
                        if beside:
                            beside(BODY * i + s)

                if beside:
                    for i in range(BODIES):
                        body(i)
                    beside()
                else:
                    body(0)
                    with dve.Fori(1, BODIES) as i:
                        body(i)

            def attn1_proj(b, t, every):
                yield t
                for i in range(BPB):
                    h = h_blk(BPB * b + i)
                    hprev = H[:, b, i * BLK:(i + 1) * BLK]
                    dve.wait_ge(s_h[b], BPB * 3)
                    link(dve.tensor_tensor(blk(xx[b], i), hprev, h, ALU.subtract))
                    dve.scalar_tensor_tensor(blk(y0[b], i), blk(xx[b], i), col(C_MAA), h, ALU.mult, ALU.add).then_inc(s_xmx, 1)
                users = [job(n) for n in ("td1", "k", "v", "r", "g")]
                f = 0
                for idx, (name, reader) in enumerate(JOBS):
                    yield t + every * idx + 1
                    if reader != "dve":
                        continue
                    for i in range(BPB):
                        at = blk(xf[b][f % 2], i)
                        if f >= 2:
                            dve.wait_ge(s_mx, BPB * (len(JOBS) * b + users[f - 2]) + i + 1)
                        dve.wait_ge(s_mx, BPB * (len(JOBS) * b + idx) + i + 1)
                        dve.scalar_tensor_tensor(at, job_bank(b, idx, i), col(C_MAA + 1 + f), blk(xx[b], i), ALU.add,
                                                 ALU.mult).then_inc(s_mxd, 1)
                        dve.wait_ge(*read_count(b, idx, i))
                        dve.tensor_tensor(at, at, h_blk(BPB * b + i), ALU.add).then_inc(s_xf, 1)
                    f += 1

            def attn1_state(b, t):
                A = A1[b]

                def outer(i, j):
                    n = SLOTS * b + HK * i + j
                    dve.wait_ge(s_vb, n + 1)
                    if n >= 2:
                        dve.wait_ge(s_S, n - 1)
                    dve.tensor_tensor(kv[n % 2], blk(A["K"], i), side(0), ALU.mult).then_inc(s_kv, 1)

                def state(i, j):
                    n = SLOTS * b + HK * i + j
                    if n >= 2:
                        dve.wait_ge(s_prod, n - 1)
                    start = 0.0
                    if i:
                        start = carry[:, j:j + 1]
                        link(dve.tensor_copy(S[n % 2][:, 0:1], start))
                    dve.wait_ge(s_kv, n + 1)
                    dve.tensor_tensor_scan(S[n % 2][:, 1:BLK + 1], blk(A["dec"], i), kv[n % 2], start, ALU.mult,
                                           ALU.add).then_inc(s_S, 1)
                    if i == 0:
                        dve.wait_ge(s_S, n + 1)
                        link(dve.tensor_copy(carry[:, j:j + 1], S[n % 2][:, BLK:BLK + 1]))

                def bonus(i):
                    dve.wait_ge(s_q, BPB * b + i + 1)
                    dve.tensor_tensor(blk(y0[b], i), blk(A["V"], i), side(0), ALU.mult).then_inc(s_y0, 1)

                def take(i):
                    dve.wait_ge(s_yps, SLOTS * b + HK * (i + 1))
                    dve.wait_ge(s_y0, BPB * b + i + 1)
                    dve.tensor_tensor(blk(yy[b], i), blk(y0[b], i), side(1), ALU.add).then_inc(s_y, 1)

                def states(i):
                    yield t + ST_BLOCK * i + 2
                    bonus(i)
                    for j in range(HK + 1):
                        yield t + ST_BLOCK * i + ST_OUTER + j
                        if j < HK:
                            outer(i, j)
                        if j:
                            state(i, j - 1)

                def takes():
                    for i in range(BPB):
                        yield t + ST_BLOCK * i + ST_TAKE
                        take(i)

                yield t
                dve.wait_ge(s_mxa, BPB * NACT * (b + 1))
                dve.wait_ge(s_mx, BPB * len(JOBS) * (b + 1))
                dve.wait_ge(s_dec, BPB * (b + 1))
                for i in range(BPB):
                    dve.scalar_tensor_tensor(blk(yy[b], i), blk(A["R"], i), col(C_U1), blk(A["K"], i), ALU.mult,
                                             ALU.mult).then_inc(s_ruk, 1)
                yield t + 1
                hi, lo = h_hi[:, b * T:(b + 1) * T], h_lo[:, b * T:(b + 1) * T]
                if b:
                    dve.wait_ge(s_prod, SLOTS * b)
                for k in range(2):
                    link(dve.memset(S[k][:, 0:1], 0.0))
                dve.tensor_copy(hi, A["V"]).then_inc(s_vsp, 1)
                dve.wait_ge(s_vsp, 2 * b + 1)
                dve.tensor_tensor(lo, A["V"], hi.bitcast(F32), ALU.subtract).then_inc(s_vsp, 1)
                yield from woven(chained(states(i) for i in range(BPB)), takes())

            def group_norm(b, t=0):
                k0 = BPB * b
                yield t + 2
                for i in range(BPB):
                    dve.wait_ge(s_gm, k0 + i + 1)
                    dve.wait_ge(s_y, BPB * (b + 1))
                    dve.tensor_tensor(blk(y0[b], i), blk(yy[b], i), side(i), ALU.subtract).then_inc(s_gc, 1)
                yield t + 5
                for i in range(BPB):
                    dve.wait_ge(s_gv, k0 + i + 1)
                    link(dve.tensor_scalar(gn_rs[:, 0, i].rearrange("p t h -> p (t h)"), side(i)[:, 0:BLK // HK],
                                           GN_EPS, None, ALU.add))
                inverse_root([gn_rs[:, n].rearrange("p k t h -> p (k t h)") for n in range(3)])
                for i in range(BPB):
                    dve.tensor_copy(blk(yy[b], i).rearrange("p (t h k) -> p t h k", h=P // HK, k=HK),
                                    gn_rs[:, 1, i].unsqueeze(3).broadcast_to([P, BLK // P, P // HK, HK])).then_inc(s_ge, 1)
                for i in range(BPB):
                    yield t + 8 + i
                    dve.wait_ge(s_gr, k0 + i + 1)
                    dve.wait_ge(s_G, k0 + i + 1)
                    link(dve.scalar_tensor_tensor(blk(y0[b], i), blk(y0[b], i), col(C_LNG), side(i), ALU.mult, ALU.mult))
                    dve.scalar_tensor_tensor(blk(y0[b], i), blk(y0[b], i), col(C_LNB), blk(A1[b]["G"], i), ALU.add,
                                             ALU.mult).then_inc(s_yn, 1)
                yield t + 11
                for i in range(BPB):
                    k = BPB * b + i
                    dve.wait_ge(s_out1, k + 1)
                    dve.scalar_tensor_tensor(blk(x, k), side(i), gate[:, 1, 0, b:b + 1], blk(x, k),
                                             ALU.mult, ALU.add).then_inc(s_xup[b], 1)

            weave(layer_norm(0, 0), modulation(), layer_norm(0, 1, 3))
            run(attn0_exponents(0))
            exponents1 = attn0_exponents(1)
            next(exponents1)
            next(exponents1)
            run(attn0_denominator(0))
            run(attn0_numerator(0))
            attn0_quotient0()
            run(exponents1)
            run(attn0_add(0))
            weave(layer_norm(1, 0), attn0_denominator(1, 1))

            def rest0():
                yield from route(0, QUICK)
                yield from start_sum(0, STEP_ACC)
                yield from attn0_numerator(1, 9)
                yield from attn0_quotient1(11)
                yield from attn0_add(1, T_OUT0 + 2)
                yield from layer_norm(1, 1, T_LN1)
                yield from route(1, [T_ROUTE1 + d for d in SLOW])
                yield from start_sum(1, T_START1 + 2)

            beside = between(rest0())
            beside(-1)
            experts(0, beside)

            def start1():
                yield from layer_norm(2, 0, T_LN2)
                yield from attn1_proj(0, T_PROJ, 1)
                yield from attn1_state(0, T_STATE0)
                yield from group_norm(0, T_GN0)

            experts(1, between(start1()), before=finish(0))
            run(finish(1))

            def join1():
                yield from layer_norm(2, 1)
                yield from attn1_proj(1, 9, 1)

            def normed0():
                yield from layer_norm(3, 0)
                yield from route(2, [13 + d for d in SLOW])

            weave(join1(), normed0())

            def rest1():
                yield from start_sum(2, 2)
                yield from attn1_state(1, T_STATE1)
                yield from group_norm(1, T_GN)
                yield from layer_norm(3, 1, T_LN3)
                yield from route(3, [T_ROUTE3 + d for d in SLOW])
                yield from start_sum(3, 63)

            dve.wait_ge(s_mx, BPB * NB * len(JOBS))
            experts(2, between(rest1()))
            experts(3, before=finish(2))
            run(finish(3))


def kernel(**inputs):
    import concourse.bacc as _bacc
    from concourse import mybir as _mybir
    from concourse.bass_utils import run_bass_kernel_spmd as _run

    I = {k: np.asarray(v) for k, v in inputs.items()}
    f32 = np.float32

    def column(a):
        return np.asarray(a).reshape(P, 1)

    cols = np.zeros((P, NCOL), f32)
    for c, name in ((C_TD0, "L0_attn_time_decay"), (C_U0, "L0_attn_time_first"), (C_MAA, "L1_attn_time_maa_x"),
                    (C_TD1, "L1_attn_time_decay"), (C_U1, "L1_attn_u"), (C_LNG, "L1_attn_ln_g"),
                    (C_LNB, "L1_attn_ln_b")):
        cols[:, c:c + 1] = column(I[name])
    for f, m in enumerate(MIXES):
        cols[:, C_MAA + 1 + f:C_MAA + 2 + f] = column(I["L1_attn_time_maa_" + m])
    cols[:, C_COND:C_COND + NB] = I["L0_c"].T
    cols[:, C_COND + NB:C_COND + 2 * NB] = I["L1_c"].T

    def expert_pack(w1, w2):
        w2 = w2.reshape(NE, NC, P, P).transpose(0, 2, 1, 3).reshape(NE, P, FH)
        return np.concatenate([w1, w2], axis=2)

    rows = np.arange(P)
    head, within = rows // HK, rows % HK
    same = (head[:, None] == head[None, :])
    consts = np.zeros((P, 19, P), f32)
    for j in range(HK):
        m = (same & (within == j)[:, None]).astype(f32)
        consts[:, j, :] = m
        consts[:, HK + j, :] = m.T
    consts[:, 16, :] = same
    consts[:, 17, :] = np.eye(P)
    consts[:, 18, 0:NT * NE] = np.tile(np.arange(NE, 0, -1), NT)

    arrays = {
        "x_t": I["L0_attn_x"].reshape(N, P).T,
        "wrvk_t": I["L0_attn_W_rvk"].T,
        "wout0_t": I["L0_attn_W_out"].T,
        "cols": cols,
        "wmod": np.stack([I["L0_wmod"], I["L1_wmod"]], axis=1),
        "experts": np.concatenate([
            expert_pack(I["L0_ffn_W1"], I["L0_ffn_W2"]),
            expert_pack(I["L1_ffn_W1"].transpose(0, 2, 1), I["L1_ffn_W2"].transpose(0, 2, 1))], axis=0),
        "b1_t": I["L0_ffn_b1"].reshape(NE * NC, P).T,
        "b2": I["L0_ffn_b2"],
        "br": I["L0_ffn_br"],
        "wr": np.stack([I["L0_ffn_Wr"], I["L1_ffn_Wr"].T], axis=1),
        "maaw1": I["L1_attn_maa_w1"],
        "maaw2": I["L1_attn_maa_w2"].reshape(5 * EMIX, P),
        "tdw1": I["L1_attn_td_w1"],
        "tdw2": I["L1_attn_td_w2"],
        "wproj_t": np.stack([I["L1_attn_W" + n].T for n in "kvrgo"], axis=1),
        "consts": consts,
    }
    nc = _bacc.Bacc("TRN2", target_bir_lowering=False, num_devices=1)
    args, feed = [], {}
    for name, a in arrays.items():
        a = np.ascontiguousarray(a)
        feed[name + "_dram"] = a
        args.append(nc.dram_tensor(name + "_dram", a.shape, _mybir.dt.from_np(a.dtype), kind="ExternalInput").ap())
    args.append(nc.dram_tensor("out_t_dram", (P, N), F32, kind="ExternalOutput").ap())
    args.append(nc.dram_tensor("gates", (HALVES, NE, T), F32, kind="Internal").ap())
    program(nc, *args)
    r = _run(nc, [feed], core_ids=[0])
    return np.ascontiguousarray(r.results[0]["out_t_dram"].T).reshape(NB, T, P)
```
